# Optimizing a Trainium2 kernel written in Bass

```python
import numpy as np
import jax
import jax.numpy as jnp

def _softmax(x, axis=-1):
    return jax.nn.softmax(x, axis=axis)

def _gelu(x):
    return jax.nn.gelu(x, approximate=True)

def _silu(x):
    return jax.nn.silu(x)

def _sigmoid(x):
    return jax.nn.sigmoid(x)

def _layernorm(x, axis=-1, eps=1e-05):
    m = jnp.mean(x, axis=axis, keepdims=True)
    v = jnp.var(x, axis=axis, keepdims=True)
    return (x - m) / jnp.sqrt(v + eps)

def _scatter_add(tgt, idx, src, axis=0):
    return tgt.at[idx].add(src)

def _segment_sum(src, seg, n):
    return jax.ops.segment_sum(src, seg, n)
kernel_name = 'mk_adj_preln_d4_adj_r2_2c1bf6'

def setup_inputs(seed: int=0):
    np.random.seed(seed)
    _w = jnp.asarray

    def _rec_inputs():
        import jax
        import jax.numpy as jnp
        _gk = jax.random.key(seed)
        x = -0.001547 + 1.001 * jax.random.normal(jax.random.fold_in(_gk, 1), (2048, 64), jnp.float32)
        _a = jax.random.bernoulli(jax.random.fold_in(_gk, 2), 0.0078125, (2048, 2048))
        _a = jnp.logical_or(_a, jnp.swapaxes(_a, -1, -2))
        _a = jnp.logical_or(_a, jnp.eye(2048, dtype=bool))
        adj = _a.astype(jnp.int32)
        return (x, adj)
    x, adj = _rec_inputs()

    def _L0_gnn_setup():
        import jax, jax.numpy as jnp
        import numpy as np
        N = 2048
        OUT = 64
        EMB = 8
        K_TAYLOR = 4
        EPS = 1e-12
        key = jax.random.key(seed)
        k1, k2, k3, k4 = jax.random.split(key, 4)
        h = jax.random.normal(k1, (N, OUT), dtype=jnp.float32)
        adj = jax.random.randint(k2, (N, N), 0, 2, dtype=jnp.int32)
        w_k = jax.random.normal(k3, (OUT, EMB), dtype=jnp.float32)
        w_q = jax.random.normal(k4, (OUT, EMB), dtype=jnp.float32)
        return {'h': h, 'adj': adj, 'w_k': w_k, 'w_q': w_q}
    _L0_gnn_all = _L0_gnn_setup()
    _L0_gnn_in = {k: v for k, v in _L0_gnn_all.items() if k in ('w_k', 'w_q')}
    del _L0_gnn_all

    def _L1_gnn_setup():
        import jax, jax.numpy as jnp
        import numpy as np
        EPS = 1e-07

        def _mobius_add(x, y):
            x2 = jnp.sum(x * x, axis=-1, keepdims=True)
            y2 = jnp.sum(y * y, axis=-1, keepdims=True)
            xy = jnp.sum(x * y, axis=-1, keepdims=True)
            num = (1.0 + 2.0 * xy + y2) * x + (1.0 - x2) * y
            den = 1.0 + 2.0 * xy + x2 * y2
            return num / jnp.maximum(den, EPS)

        def _lambda_x(x):
            return 2.0 / jnp.clip(1.0 - jnp.sum(x * x, axis=-1, keepdims=True), EPS, None)

        def _logmap(y, x):
            u = _mobius_add(-x, y)
            un = jnp.clip(jnp.linalg.norm(u, axis=-1, keepdims=True), EPS, 1.0 - 1e-05)
            return 2.0 / _lambda_x(x) * jnp.arctanh(un) * (u / un)

        def _expmap(v, x):
            vn = jnp.clip(jnp.linalg.norm(v, axis=-1, keepdims=True), EPS, None)
            second = jnp.tanh(_lambda_x(x) * vn * 0.5) * (v / vn)
            return _mobius_add(x, second)
        key = jax.random.key(seed)
        k1, k2 = jax.random.split(key)
        N, D = (512, 64)
        u = jax.random.normal(k1, (N, D), dtype=jnp.float32)
        x = 0.5 * u / (1.0 + jnp.linalg.norm(u, axis=-1, keepdims=True))
        adj = jax.random.randint(k2, (N, N), 0, 2, dtype=jnp.int32)
        return {'x': x, 'adj': adj}
    _L1_gnn_all = _L1_gnn_setup()
    _L1_gnn_in = {k: v for k, v in _L1_gnn_all.items() if k in ()}
    del _L1_gnn_all

    def _L2_gnn_setup():
        import jax, jax.numpy as jnp
        import numpy as np
        ALPHA = 0.2
        NEG_INF = -9000000000000000.0
        key = jax.random.key(seed)
        k1, k2, k3, k4 = jax.random.split(key, 4)
        N, F_IN, F_OUT = (512, 64, 64)
        h = jax.random.normal(k1, (N, F_IN), dtype=jnp.float32)
        adj = jax.random.randint(k2, (N, N), 0, 2, dtype=jnp.int32)
        lim_W = 1.414 * np.sqrt(6.0 / (F_IN + F_OUT))
        W = jax.random.uniform(k3, (F_IN, F_OUT), minval=-lim_W, maxval=lim_W, dtype=jnp.float32)
        lim_a = 1.414 * np.sqrt(6.0 / (2 * F_OUT + 1))
        a = jax.random.uniform(k4, (2 * F_OUT, 1), minval=-lim_a, maxval=lim_a, dtype=jnp.float32)
        return {'h': h, 'adj': adj, 'W': W, 'a': a}
    _L2_gnn_all = _L2_gnn_setup()
    _L2_gnn_in = {k: v for k, v in _L2_gnn_all.items() if k in ('W', 'a')}
    del _L2_gnn_all

    def _L3_gnn_setup():
        import jax, jax.numpy as jnp
        import numpy as np
        N = 10000
        F = 64
        O = 64
        key = jax.random.key(seed)
        k1, k2, k3 = jax.random.split(key, 3)
        x = jax.random.normal(k1, (N, F), dtype=jnp.float32)
        adj = jax.random.randint(k2, (N, N), 0, 2, dtype=jnp.int32)
        stdv = float(np.sqrt(6.0 / (2 * F + O)))
        weight = jax.random.uniform(k3, (2 * F, O), dtype=jnp.float32, minval=-stdv, maxval=stdv)
        bias = jnp.zeros((O,), dtype=jnp.float32)
        return {'x': x, 'adj': adj, 'weight': weight, 'bias': bias}
    _L3_gnn_all = _L3_gnn_setup()
    _L3_gnn_in = {k: v for k, v in _L3_gnn_all.items() if k in ('weight', 'bias')}
    del _L3_gnn_all
    return {'x': x, 'adj': adj, 'L0_gnn_w_k': _L0_gnn_in['w_k'], 'L0_gnn_w_q': _L0_gnn_in['w_q'], 'L2_gnn_W': _L2_gnn_in['W'], 'L2_gnn_a': _L2_gnn_in['a'], 'L3_gnn_weight': _L3_gnn_in['weight'], 'L3_gnn_bias': _L3_gnn_in['bias']}

def reference(x, adj, L0_gnn_w_k, L0_gnn_w_q, L2_gnn_W, L2_gnn_a, L3_gnn_weight, L3_gnn_bias):
    import jax
    import jax.numpy as jnp

    def _L0_gnn_ref(h, adj, w_k, w_q):
        import jax, jax.numpy as jnp
        import numpy as np
        N = 2048
        OUT = 64
        EMB = 8
        K_TAYLOR = 4
        EPS = 1e-12
        h = h - h.mean(axis=-1, keepdims=True)
        h = h / jnp.maximum(jnp.linalg.norm(h, axis=-1, keepdims=True), EPS)
        k = h @ w_k
        q = h @ w_q
        scores = k @ q.T / jnp.sqrt(jnp.float32(EMB))
        a_att = jax.nn.softmax(scores, axis=-1)
        a = adj.astype(jnp.float32) * a_att
        a = a / a.sum(axis=-1, keepdims=True)
        result = a
        fact = 1.0
        for i in range(2, K_TAYLOR):
            a = a @ a
            fact = fact * i
            result = result + a / fact
        return result @ h

    def _L1_gnn_ref(x, adj):
        import jax, jax.numpy as jnp
        import numpy as np
        EPS = 1e-07

        def _mobius_add(x, y):
            x2 = jnp.sum(x * x, axis=-1, keepdims=True)
            y2 = jnp.sum(y * y, axis=-1, keepdims=True)
            xy = jnp.sum(x * y, axis=-1, keepdims=True)
            num = (1.0 + 2.0 * xy + y2) * x + (1.0 - x2) * y
            den = 1.0 + 2.0 * xy + x2 * y2
            return num / jnp.maximum(den, EPS)

        def _lambda_x(x):
            return 2.0 / jnp.clip(1.0 - jnp.sum(x * x, axis=-1, keepdims=True), EPS, None)

        def _logmap(y, x):
            u = _mobius_add(-x, y)
            un = jnp.clip(jnp.linalg.norm(u, axis=-1, keepdims=True), EPS, 1.0 - 1e-05)
            return 2.0 / _lambda_x(x) * jnp.arctanh(un) * (u / un)

        def _expmap(v, x):
            vn = jnp.clip(jnp.linalg.norm(v, axis=-1, keepdims=True), EPS, None)
            second = jnp.tanh(_lambda_x(x) * vn * 0.5) * (v / vn)
            return _mobius_add(x, second)
        mask = adj > 0
        logs = jax.vmap(lambda xi: _logmap(x, xi))(x)
        v = jnp.sum(jnp.where(mask[..., None], logs, 0.0), axis=1)
        return _expmap(v, x)

    def _L2_gnn_ref(h, adj, W, a):
        import jax, jax.numpy as jnp
        import numpy as np
        ALPHA = 0.2
        NEG_INF = -9000000000000000.0
        F_OUT = W.shape[1]
        Wh = h @ W
        a1, a2 = (a[:F_OUT, 0], a[F_OUT:, 0])
        e = (Wh @ a1)[:, None] + (Wh @ a2)[None, :]
        e = jax.nn.leaky_relu(e, negative_slope=ALPHA)
        scores = jnp.where(adj > 0, e, jnp.float32(NEG_INF))
        attention = jax.nn.softmax(scores, axis=1)
        h_prime = attention @ Wh
        return jax.nn.elu(h_prime)

    def _L3_gnn_ref(x, adj, weight, bias):
        import jax, jax.numpy as jnp
        import numpy as np
        N = 10000
        F = 64
        O = 64
        a = (adj == 1).astype(x.dtype)
        deg = jnp.sum(a, axis=1, keepdims=True)
        x1 = a @ x / deg
        n_x = jnp.concatenate([x1, x], axis=1)
        return n_x @ weight + bias
    h = jnp.maximum(_layernorm(x, axis=-1), 0.0)
    x = x + _L0_gnn_ref(h, adj, L0_gnn_w_k, L0_gnn_w_q)
    h = jnp.maximum(_layernorm(x, axis=-1), 0.0)
    x = x + _L1_gnn_ref(h, adj)
    h = jnp.maximum(_layernorm(x, axis=-1), 0.0)
    x = x + _L2_gnn_ref(h, adj, L2_gnn_W, L2_gnn_a)
    h = jnp.maximum(_layernorm(x, axis=-1), 0.0)
    x = x + _L3_gnn_ref(h, adj, L3_gnn_weight, L3_gnn_bias)
    return x

_drawn_inputs = setup_inputs


def setup_inputs(seed=0):
    import zlib

    import numpy as np

    out = dict(_drawn_inputs(seed))
    spreads = {'L3_gnn_bias': (0.0, 0.1)}
    factors = {}
    for name, (base, spread) in spreads.items():
        noise = np.random.default_rng([zlib.crc32(name.encode()), seed]).standard_normal(out[name].shape)
        drawn = base * np.exp(spread * noise) if base else spread * noise
        out[name] = jnp.asarray(drawn.astype(out[name].dtype))
    for name, factor in factors.items():
        out[name] = (out[name] * factor).astype(out[name].dtype)
    return out
```

```python
from contextlib import ExitStack

import concourse.bass as bass
from concourse import mybir

P = 128
N = 2048
D = 64
T = N // P
EMB = 8
CH = 512
NC = N // CH
TC = CH // P
KP = 9 * EMB
MROW = 96
KM = MROW + 3
AUG = D + 2
PER_BANK = 7
LN_EPS = 1e-5
EPS0 = 1e-12
EPS1 = 1e-7
UMAX = 1.0 - 1e-5
DMIN = 1e-9
ALPHA = 0.2

F32 = mybir.dt.float32
BF16 = mybir.dt.bfloat16
F8 = mybir.dt.float8e4
I32 = mybir.dt.int32
ALU = mybir.AluOpType
ACT = mybir.ActivationFunctionType
X = mybir.AxisListType.X

TRI = [(j, i) for j in range(T) for i in range(j, T)]
CHUNKS = [TRI[c:c + TC] for c in range(0, len(TRI), TC)]
NCH = len(CHUNKS)


def runs(chunk, diagonal):
    out = []
    for s, (j, i) in enumerate(chunk):
        if i == j and not diagonal:
            continue
        if out and out[-1][2] == j and out[-1][0] + out[-1][1] == s:
            out[-1][1] += 1
        else:
            out.append([s, 1, j, i])
    return out


def build(nc, x, adj_t, w_k, w_q, w2, w2_t, a2, w3, bias3, sel, ident, out):
    ctx = ExitStack()
    with ctx:
        def sb(name, shape, dt=F32):
            return ctx.enter_context(nc.sbuf_tensor(name, shape, dt))

        def sem(name):
            return ctx.enter_context(nc.semaphore(name))

        ps = ctx.enter_context(nc.psum_tensor("ps", [P, 8, CH], F32))

        big = sb("big", [P, T * N])
        mask8 = sb("mask8", [P, T, N], F8)
        ht = sb("ht", [P, N])
        scratch = sb("scratch", [P, N])
        k_part = sb("k_part", [P, N], BF16)
        q_part = sb("q_part", [P, N], BF16)
        rounded = sb("rounded", [P, N], BF16)
        xs = sb("xs", [P, T, D])
        feat = sb("feat", [P, T, AUG])
        idf = sb("idf", [P, P])
        idb = sb("idb", [P, P], BF16)
        wk_rep = sb("wk_rep", [D, 9, EMB])
        wq_rep = sb("wq_rep", [D, 9, EMB])
        wkq = sb("wkq", [D, 2, EMB])
        sel_sb = sb("sel_sb", [P, 4])
        w2_sb = sb("w2_sb", [D, AUG])
        w2t_sb = sb("w2t_sb", [D, D])
        a2_sb = sb("a2_sb", [D, 2])
        w3_sb = sb("w3_sb", [D, 2, D])
        bias_sb = sb("bias_sb", [P, D])
        st = sb("st", [P, 24, T])
        rowmax = sb("rowmax", [P, T, 2])
        m_parts = sb("m_parts", [P, T, 3], BF16)
        half_col = sb("half_col", [P, 2])

        attn = big[:, :].rearrange("p (j i) -> p j i", j=T)
        adj_stage = big[:, :].bitcast(I32).rearrange("p (j i) -> p j i", j=T)
        u_buf = [ht[:, b * T * D:(b + 1) * T * D].rearrange("p (t f) -> p t f", t=T) for b in range(2)]
        xc = scratch[:, 0:T * D].rearrange("p (t f) -> p t f", t=T)
        sq = scratch[:, T * D:2 * T * D].rearrange("p (t f) -> p t f", t=T)
        h_feat = feat[:, :, 0:D]

        cut = [0]

        def carve(n):
            cut[0] += n
            return big[:, cut[0] - n:cut[0]]
        feat_a = carve(T * AUG).rearrange("p (t f) -> p t f", t=T)
        feat_b = carve(T * AUG).rearrange("p (t f) -> p t f", t=T)
        xt, xa, xb = carve(N), carve(N), carve(N)
        ring = {n: [carve(CH) for _ in range(3)] for n in
                ("den", "dist", "prod", "inv_s", "un", "lnp", "lnm", "atn", "w", "w_up", "w_lo")}
        agg = carve(T * AUG).rearrange("p (t f) -> p t f", t=T)
        assert cut[0] <= T * N
        cut[0] = 0
        row_1, row_2, best = carve(N), carve(N), carve(N)
        p_ring = [carve(N) for _ in range(3)]
        wh = carve(T * AUG).rearrange("p (t f) -> p t f", t=T)
        assert cut[0] <= T * N
        cut[0] = 0
        agg2 = carve(T * AUG).rearrange("p (t f) -> p t f", t=T)
        self3 = carve(T * D).rearrange("p (t f) -> p t f", t=T)
        r3 = carve(T * D).rearrange("p (t f) -> p t f", t=T)
        PW = 3 * D + 1
        parts3 = carve(T * (PW + 1) // 2).bitcast(BF16)[:, 0:T * PW].rearrange("p (t f) -> p t f", t=T)
        assert cut[0] <= 6 * N

        def stat(n):
            return st[:, n, :]

        def over_features(ap, width=D):
            return ap.unsqueeze(2).to_broadcast([P, T, width])

        names = """x_in w_in const_set adj_cast var_ready std_ready feat_ready tr_ready ht_ready
        rep_ready rnd_ready part_ready gmax_ready gmax_read mcol_ready mrow_ready mrow_set score_ready
        exp_ready masked_v masked_g prod0_ready prod0_read prop_ready layer0_done
        t1_ready xt_ready xa_ready gram_ready gram_read p_ready invs_ready un_ready ln_ready atn_ready
        w_ready wt_ready wlo_ready wup_ready sum1_done step lift_ready wa_ready wh_ready wh_read ab_ready
        best_ready bt_ready m_ready rows_ready row1_set z_ready pe_ready pm_ready sum2_done elu_ready
        elu_exp h3_ready h3_read parts_ready sum3_ready sum3_read y_ready out_done
        min_ready min_t min_r min_b norm_a norm_b tanh_a tanh_b wa_set layer1_done xin_ready""".split()
        S = {n: sem(n) for n in names}
        adj_in = [sem(f"adj_in_{j}") for j in range(T)]

        block = ctx.enter_context(nc.Block())

        def acc_1(t, width=AUG):
            return ps[:, 5 + t // PER_BANK, (t % PER_BANK) * width:(t % PER_BANK + 1) * width]

        SLOT, ORDER = {}, []

        def plan(kind, c):
            for g in range(8 * c, 8 * c + 8):
                SLOT[kind, g] = len(ORDER) % 3
                ORDER.append((kind, g))
        for c in range(NC + 1):
            if c < NC:
                plan("max", c)
            if c >= 1:
                plan("score", c - 1)

        def bias_one():
            return half_col[0:1, 0:1].to_broadcast([1, P])

        @block.sync
        def _(sp):
            sp.dma_start(xs[:, :, :], x.rearrange("(t p) f -> p t f", p=P)).then_inc(S["x_in"], 16)
            for dst, src in ((idf[:, :], ident), (sel_sb[:, :], sel), (wkq[:, 0, :], w_k), (wkq[:, 1, :], w_q),
                             (w2_sb[:, 0:D], w2), (w2t_sb[:, :], w2_t), (a2_sb[:, :], a2),
                             (w3_sb[:, :, :], w3.rearrange("(s k) f -> k s f", s=2)),
                             (bias_sb[:, :], bias3.partition_broadcast(P))):
                sp.dma_start(dst, src).then_inc(S["w_in"], 16)
            for j in range(T):
                sp.dma_start(adj_stage[:, j, :], adj_t[j * P:(j + 1) * P, :]).then_inc(adj_in[j], 16)
            for h in range(2):
                sp.wait_ge(S["y_ready"], h + 1)
                sp.dma_start(out.rearrange("(t p) f -> p t f", p=P)[:, h * 8:h * 8 + 8, :],
                             xs[:, h * 8:h * 8 + 8, :]).then_inc(S["out_done"], 16)
            sp.wait_ge(S["out_done"], 32)

        W_IN = 16 * 9

        @block.gpsimd
        def _(pool):
            nc.gpsimd.memset(k_part[:, :], 0.0).then_inc(S["const_set"], 1)
            nc.gpsimd.memset(q_part[:, :], 0.0).then_inc(S["const_set"], 1)
            nc.gpsimd.memset(feat[:, :, D:D + 1], 1.0).then_inc(S["const_set"], 1)
            nc.gpsimd.memset(half_col[:, :], 1.0).then_inc(S["const_set"], 1)
            pool.wait_ge(S["const_set"], 4)
            nc.gpsimd.memset(q_part[MROW:KM, :], -1.0).then_inc(S["const_set"], 1)
            pool.wait_ge(S["const_set"], 5)
            for j in range(T):
                pool.wait_ge(adj_in[j], 16)
                nc.gpsimd.tensor_copy(mask8[:, j, :], adj_stage[:, j, :], saturate=False)\
                    .then_inc(S["adj_cast"], 1)
            for c in range(NC):
                for g in (6, 7):
                    pool.wait_ge(S["exp_ready"], 8 * c + g + 1)
                    e = attn[:, 2 * g:2 * g + 2, c * CH:(c + 1) * CH]
                    nc.gpsimd.tensor_tensor(e, e, mask8[:, 2 * g:2 * g + 2, c * CH:(c + 1) * CH],
                                            ALU.mult).then_inc(S["masked_g"], 1)
            for c in range(NCH + 2):
                if c < NCH:
                    pool.wait_ge(S["ln_ready"], c + 1)
                    if c >= 3:
                        pool.wait_ge(S["w_ready"], c - 2)
                    nc.gpsimd.tensor_tensor(ring["atn"][c % 3], ring["lnp"][c % 3], ring["lnm"][c % 3],
                                            ALU.subtract).then_inc(S["atn_ready"], 1)
                if c >= 2:
                    b = c - 2
                    pool.wait_ge(S["w_ready"], b + 1)
                    if b >= 3:
                        pool.wait_ge(S["sum1_done"], b - 2)
                    for s, n, j, i in runs(CHUNKS[b], True):
                        nc.gpsimd.tensor_tensor(ring["w_up"][b % 3][:, s * P:(s + n) * P],
                                                ring["w"][b % 3][:, s * P:(s + n) * P],
                                                mask8[:, j, i * P:(i + n) * P], ALU.mult).then_inc(S["wup_ready"], 1)

        wup_count = [0]
        for ch in CHUNKS:
            wup_count.append(wup_count[-1] + len(runs(ch, True)))

        @block.scalar
        def _(act):
            def root(ready, value, dst, src, done):
                act.wait_ge(S[ready], value)
                nc.scalar.activation(dst, src, ACT.Sqrt).then_inc(S[done], 1)

            def transposed(tr0):
                for g in range(NC):
                    act.wait_ge(S["tr_ready"], tr0 + g + 1)
                    nc.scalar.copy(ht[0:D, g * CH:(g + 1) * CH], ps[0:D, g, :]).then_inc(S["ht_ready"], 1)

            root("var_ready", 1, stat(3), stat(2), "std_ready")
            root("var_ready", 2, stat(3), stat(2), "std_ready")
            transposed(0)
            for n in range(2):
                act.wait_ge(S["rep_ready"], n + 1)
                if n:
                    act.wait_ge(S["part_ready"], 2)
                nc.scalar.copy(rounded[0:KP, :].rearrange("p (b c) -> p b c", b=NC),
                               ps[0:KP, 4 * n:4 * n + 4, :]).then_inc(S["rnd_ready"], 1)
                act.wait_ge(S["part_ready"], 2 * n + 1)
                nc.scalar.copy(rounded[0:KP, :], scratch[0:KP, :]).then_inc(S["rnd_ready"], 1)
            for c in range(NC):
                act.wait_ge(S["mrow_ready"], c + 1)
                nc.scalar.copy(k_part[MROW:KM, c * CH:(c + 1) * CH], ps[MROW:KM, 7, :]).then_inc(S["mrow_set"], 1)
                for g in range(8):
                    act.wait_ge(S["score_ready"], 8 * c + g + 1)
                    if c == 0:
                        act.wait_ge(S["adj_cast"], 2 * g + 2)
                    b = 2 * SLOT["score", 8 * c + g]
                    nc.scalar.activation(attn[:, 2 * g:2 * g + 2, c * CH:(c + 1) * CH], ps[:, b:b + 2, :],
                                         ACT.Exp, scale=EMB ** -0.5).then_inc(S["exp_ready"], 1)
            root("var_ready", 3, stat(3), stat(2), "std_ready")
            for g in range(NC):
                act.wait_ge(S["t1_ready"], 3 * g + 1)
                nc.scalar.copy(xt[0:AUG, g * CH:(g + 1) * CH], ps[0:AUG, 0, :]).then_inc(S["xt_ready"], 1)
                act.wait_ge(S["t1_ready"], 3 * g + 3)
                nc.scalar.copy(xb[0:AUG, g * CH:(g + 1) * CH], ps[0:AUG, 2, :]).then_inc(S["xt_ready"], 1)
            for c in range(NCH + 1):
                if c < NCH:
                    act.wait_ge(S["p_ready"], c + 1)
                    nc.scalar.activation(ring["prod"][c % 3], ring["prod"][c % 3], ACT.Ln).then_inc(S["lift_ready"], 1)
                    act.wait_ge(S["lift_ready"], c + 1)
                    if c >= 3:
                        act.wait_ge(S["w_ready"], c - 2)
                    nc.scalar.activation(ring["inv_s"][c % 3], ring["prod"][c % 3], ACT.Exp,
                                         scale=-0.5).then_inc(S["invs_ready"], 1)
                if c >= 1:
                    b = c - 1
                    act.wait_ge(S["un_ready"], b + 1)
                    if b >= 3:
                        act.wait_ge(S["atn_ready"], b - 2)
                    nc.scalar.activation(ring["lnp"][b % 3], ring["un"][b % 3], ACT.Ln, bias=half_col[:, 1:2])
                    nc.scalar.activation(ring["lnm"][b % 3], ring["un"][b % 3], ACT.Ln, bias=half_col[:, 1:2],
                                         scale=-1.0).then_inc(S["ln_ready"], 1)
            root("norm_a", 1, stat(8), stat(7), "norm_b")
            act.wait_ge(S["tanh_a"], 1)
            nc.scalar.activation(stat(11), stat(10), ACT.Tanh).then_inc(S["tanh_b"], 1)
            root("var_ready", 4, stat(3), stat(2), "std_ready")
            transposed(4)
            act.wait_ge(S["rows_ready"], 1)
            nc.scalar.copy(row_1.rearrange("p (b c) -> p b c", b=NC), ps[:, 0:NC, :]).then_inc(S["row1_set"], 1)
            for j in range(T):
                act.wait_ge(S["z_ready"], j + 1)
                nc.scalar.activation(p_ring[j % 3], p_ring[j % 3], ACT.Exp,
                                     bias=st[:, 17, j:j + 1]).then_inc(S["pe_ready"], 1)
            act.wait_ge(S["elu_ready"], 1)
            nc.scalar.activation(sq, sq, ACT.Exp).then_inc(S["elu_exp"], 1)
            root("var_ready", 5, stat(3), stat(2), "std_ready")
            transposed(8)

        @block.tensor
        def _(pe):
            def transposes(src, g, bank, width):
                for k in range(TC):
                    last = nc.tensor.transpose(ps[0:width, bank, k * P:(k + 1) * P], src[:, TC * g + k, :], idf[:, :])
                return last

            pe.wait_ge(S["w_in"], W_IN)
            pe.wait_ge(S["feat_ready"], 1)
            for g in range(NC):
                transposes(h_feat, g, g, D).then_inc(S["tr_ready"], 1)
            pe.wait_ge(S["wa_set"], 1)
            for n, w in enumerate((wk_rep, wq_rep)):
                for g in range(NC):
                    pe.wait_ge(S["ht_ready"], g + 1 if n else NC)
                    last = nc.tensor.matmul(ps[0:KP, 4 * n + g, :], w[:, :, :], ht[0:D, g * CH:(g + 1) * CH],
                                            start=True, stop=True)
                last.then_inc(S["rep_ready"], 1)
            pe.wait_ge(S["part_ready"], 4)

            def group(kind, n):
                at = ORDER.index((kind, n))
                if at >= 3:
                    k, m = ORDER[at - 3]
                    pe.wait_ge(S["gmax_read" if k == "max" else "exp_ready"], m + 1)
                b = 2 * SLOT[kind, n]
                for h in range(2):
                    if kind == "max":
                        t, q = n // 2, 2 * (n % 2) + h
                        last = nc.tensor.matmul(ps[:, b + h, :], k_part[0:KP, t * P:(t + 1) * P],
                                                q_part[0:KP, q * CH:(q + 1) * CH], start=True, stop=True)
                    else:
                        c, j = n // 8, 2 * (n % 8) + h
                        last = nc.tensor.matmul(ps[:, b + h, :], q_part[0:KM, j * P:(j + 1) * P],
                                                k_part[0:KM, c * CH:(c + 1) * CH], start=True, stop=True)
                last.then_inc(S["gmax_ready" if kind == "max" else "score_ready"], 1)

            def propagate(k, c, width):
                n = NC * (k - 1) + c
                bank = 6 if k == 1 else 7 - c % 2
                if k == 1 and c >= 1:
                    pe.wait_ge(S["prod0_read"], n)
                elif k > 1:
                    if n >= 2:
                        pe.wait_ge(S["prod0_read"], n - 1)
                if k == 1:
                    pe.wait_ge(S["masked_v"], 6 * (c + 1))
                    pe.wait_ge(S["masked_g"], 2 * (c + 1))
                for t in range(TC):
                    o = ps[:, bank, t * width:(t + 1) * width]
                    for j in range(T):
                        if k > 1 and c == 0 and t == 0 and j % TC == 0:
                            pe.wait_ge(S["prod0_read"], NC * (k - 2) + j // TC + 1)
                        src = feat[:, j, 0:D + 1] if k == 1 else u_buf[k % 2][:, j, :]
                        last = nc.tensor.matmul(o, attn[:, j, (TC * c + t) * P:(TC * c + t + 1) * P], src,
                                                start=(j == 0), stop=(j == T - 1))
                last.then_inc(S["prod0_ready"], 1)

            for c in range(NC + 2):
                if c < NC:
                    for g in range(8 * c, 8 * c + 8):
                        group("max", g)
                if 1 <= c <= NC:
                    pe.wait_ge(S["mcol_ready"], c)
                    if c > 1:
                        pe.wait_ge(S["mrow_set"], c - 1)
                    for k in range(TC):
                        last = nc.tensor.matmul(ps[MROW:KM, 7, k * P:(k + 1) * P], m_parts[:, TC * (c - 1) + k, :],
                                                idb[:, :], start=True, stop=True)
                    last.then_inc(S["mrow_ready"], 1)
                    pe.wait_ge(S["mrow_set"], c)
                    for g in range(8 * c - 8, 8 * c):
                        group("score", g)
                if c >= 2:
                    propagate(1, c - 2, D + 1)
            for k in (2, 3, 4):
                for c in range(NC):
                    propagate(k, c, D)

            pe.wait_ge(S["feat_ready"], 2)
            for g in range(NC):
                for n, src in enumerate((feat, feat_a, feat_b)):
                    if g:
                        pe.wait_ge(S["xa_ready"] if n == 1 else S["xt_ready"], g if n == 1 else 2 * g - 1 + n // 2)
                    transposes(src, g, n, AUG).then_inc(S["t1_ready"], 1)
            pe.wait_ge(S["xt_ready"], 2 * NC)
            pe.wait_ge(S["xa_ready"], NC)

            def gram(c):
                if c >= 2:
                    pe.wait_ge(S["gram_read"], c - 1)
                for n, lhs in enumerate((xa, xb)):
                    for s, k, j, i in runs(CHUNKS[c], True):
                        last = nc.tensor.matmul(ps[:, 2 * (c % 2) + n, s * P:(s + k) * P], lhs[0:AUG, j * P:(j + 1) * P],
                                                xt[0:AUG, i * P:(i + k) * P], start=True, stop=True)
                last.then_inc(S["gram_ready"], 1)

            opened = set()

            def add_to(t, w, src):
                bank = t // PER_BANK
                first = bank not in opened
                opened.add(bank)
                return nc.tensor.matmul(acc_1(t), w, src, start=first, stop=True, skip_group_check=True)

            for c in range(NCH + 3):
                if c == 0:
                    gram(0)
                if c + 1 < NCH:
                    gram(c + 1)
                if 2 <= c < NCH + 2:
                    b = c - 2
                    pe.wait_ge(S["w_ready"], b + 1)
                    if b >= 1:
                        pe.wait_ge(S["wlo_ready"], b)
                    last = None
                    for s, (j, i) in enumerate(CHUNKS[b]):
                        if i != j:
                            last = nc.tensor.transpose(ps[:, 4, s * P:(s + 1) * P],
                                                       ring["w"][b % 3][:, s * P:(s + 1) * P], idf[:, :])
                    if last is None:
                        pe.sem_inc(S["wt_ready"], 1)
                    else:
                        last.then_inc(S["wt_ready"], 1)
                if c >= 3:
                    b = c - 3
                    pe.wait_ge(S["wup_ready"], wup_count[b + 1])
                    pe.wait_ge(S["wlo_ready"], b + 1)
                    for s, (j, i) in enumerate(CHUNKS[b]):
                        last = add_to(i, ring["w_up"][b % 3][:, s * P:(s + 1) * P], feat[:, j, :])
                        if i != j:
                            last = add_to(j, ring["w_lo"][b % 3][:, s * P:(s + 1) * P], feat[:, i, :])
                    last.then_inc(S["sum1_done"], 1)

            nc.tensor.matmul(ps[0:D, 4, 0:2], w2t_sb[:, :], a2_sb[:, :], start=True, stop=True)\
                .then_inc(S["wa_ready"], 1)
            pe.wait_ge(S["feat_ready"], 3)
            for g in range(NC):
                transposes(h_feat, g, g, D).then_inc(S["tr_ready"], 1)
            pe.wait_ge(S["wa_set"], 2)
            for g in range(NC):
                pe.wait_ge(S["ht_ready"], NC + g + 1)
                for k in range(TC):
                    t = TC * g + k
                    last = nc.tensor.matmul(acc_1(t), ht[0:D, t * P:(t + 1) * P], w2_sb[:, :],
                                            start=True, stop=True)
            last.then_inc(S["wh_ready"], 1)
            pe.wait_ge(S["min_ready"], 1)
            nc.tensor.transpose(ps[0:1, 4, 0:P], stat(18)[:, 0:1], idf[:, :]).then_inc(S["min_t"], 1)
            pe.wait_ge(S["min_r"], 1)
            nc.tensor.matmul(ps[:, 4, P:P + 1], bias_one(), st[0:1, 18, 1:2], start=True, stop=True)\
                .then_inc(S["min_b"], 1)
            pe.wait_ge(S["best_ready"], 1)
            for t in range(T):
                last = nc.tensor.transpose(ps[:, t // TC, (t % TC) * P:(t % TC + 1) * P],
                                           best[:, t * P:(t + 1) * P], idf[:, :])
            last.then_inc(S["bt_ready"], 1)
            pe.wait_ge(S["m_ready"], 1)
            for n in range(2):
                for t in range(T):
                    last = nc.tensor.matmul(ps[:, 4 * n + t // TC, (t % TC) * P:(t % TC + 1) * P],
                                            st[:, 20 + n, t:t + 1].to_broadcast([P, P]), idf[:, :],
                                            start=True, stop=True)
                last.then_inc(S["rows_ready"], 1)
            pe.wait_ge(S["row1_set"], 2)
            for j in range(T):
                pe.wait_ge(S["pm_ready"], j + 1)
                for t in range(T):
                    last = nc.tensor.matmul(acc_1(t, D + 1), p_ring[j % 3][:, t * P:(t + 1) * P], wh[:, j, 0:D + 1],
                                            start=(j == 0 and t % PER_BANK == 0), stop=True, skip_group_check=True)
                last.then_inc(S["sum2_done"], 1)

            pe.wait_ge(S["feat_ready"], 4)
            for g in range(NC):
                transposes(h_feat, g, g, D).then_inc(S["tr_ready"], 1)
            for g in range(NC):
                pe.wait_ge(S["ht_ready"], 2 * NC + g + 1)
                for k in range(TC):
                    t = TC * g + k
                    last = nc.tensor.matmul(ps[:, 4 + g, k * P:(k + 1) * P], ht[0:D, t * P:(t + 1) * P],
                                            w3_sb[:, :, :], start=True, stop=True)
            last.then_inc(S["h3_ready"], 1)
            pe.wait_ge(S["parts_ready"], 1)
            for g in range(T // 2):
                if g >= 4:
                    pe.wait_ge(S["sum3_read"], g - 3)
                for h in range(2):
                    t = 2 * g + h
                    for j in range(T):
                        last = nc.tensor.matmul(ps[:, g % 4, h * PW:(h + 1) * PW], mask8[:, j, t * P:(t + 1) * P],
                                                parts3[:, j, :], start=(j == 0), stop=(j == T - 1))
                last.then_inc(S["sum3_ready"], 1)

        @block.vector
        def _(v):
            dve = nc.vector
            done = [0]

            def step(ins):
                done[0] += 1
                ins.then_inc(S["step"], 1)
                v.wait_ge(S["step"], done[0])

            def centre(src):
                step(dve.tensor_reduce(stat(0), src, X, ALU.add))
                step(dve.tensor_scalar(stat(1), stat(0), -1.0 / D, None, ALU.mult))
                step(dve.tensor_tensor(xc, src, over_features(stat(1)), ALU.add))
                step(dve.tensor_tensor(sq, xc, xc, ALU.mult))
                step(dve.tensor_reduce(stat(0), sq, X, ALU.add))

            def layer_norm(n):
                centre(xs[:, :, :])
                dve.tensor_scalar(stat(2), stat(0), 1.0 / D, LN_EPS, ALU.mult, ALU.add).then_inc(S["var_ready"], 1)
                v.wait_ge(S["std_ready"], n)
                step(dve.reciprocal(stat(4), stat(3)))
                step(dve.tensor_tensor(xc, xc, over_features(stat(4)), ALU.mult))

            v.wait_ge(S["w_in"], W_IN)
            v.wait_ge(S["const_set"], 5)
            step(dve.tensor_copy(wk_rep[:, :, :], wkq[:, 0:1, :].to_broadcast([D, 9, EMB])))
            step(dve.tensor_copy(idb[:, :], idf[:, :]))
            dve.tensor_copy(wq_rep[:, :, :], wkq[:, 1:2, :].to_broadcast([D, 9, EMB])).then_inc(S["wa_set"], 1)
            v.wait_ge(S["x_in"], 16)
            layer_norm(1)
            step(dve.tensor_scalar(h_feat, xc, 0.0, None, ALU.max))
            centre(h_feat)
            dve.tensor_scalar(stat(2), stat(0), EPS0 * EPS0, None, ALU.max).then_inc(S["var_ready"], 1)
            v.wait_ge(S["std_ready"], 2)
            step(dve.reciprocal(stat(4), stat(3)))
            dve.tensor_tensor(h_feat, xc, over_features(stat(4)), ALU.mult).then_inc(S["feat_ready"], 1)
            v.wait_ge(S["feat_ready"], 1)
            for n, part in enumerate((k_part, q_part)):
                v.wait_ge(S["rnd_ready"], 2 * n + 1)
                dve.scalar_tensor_tensor(scratch[0:KP, :].rearrange("p (b c) -> p b c", b=NC),
                                         rounded[0:KP, :].rearrange("p (b c) -> p b c", b=NC),
                                         sel_sb[0:KP, 2 * n:2 * n + 1], ps[0:KP, 4 * n:4 * n + 4, :],
                                         ALU.mult, ALU.add).then_inc(S["part_ready"], 1)
                v.wait_ge(S["rnd_ready"], 2 * n + 2)
                dve.scalar_tensor_tensor(part[0:KP, :], rounded[0:KP, :], sel_sb[0:KP, 2 * n + 1:2 * n + 2],
                                         scratch[0:KP, :], ALU.mult, ALU.add).then_inc(S["part_ready"], 1)

            def row_max(c):
                for g in range(8 * c, 8 * c + 8):
                    v.wait_ge(S["gmax_ready"], g + 1)
                    b = 2 * SLOT["max", g]
                    dve.tensor_reduce(rowmax[:, g // 2, g % 2:g % 2 + 1], ps[:, b:b + 2, :],
                                      mybir.AxisListType.XY, ALU.max).then_inc(S["gmax_read"], 1)
                v.wait_ge(S["gmax_read"], 8 * c + 8)
                a = slice(TC * c, TC * c + TC)
                step(dve.tensor_reduce(st[:, 5, a], rowmax[:, a, :], X, ALU.max))
                step(dve.tensor_copy(m_parts[:, a, 0], st[:, 5, a]))
                step(dve.tensor_tensor(st[:, 5, a], st[:, 5, a], m_parts[:, a, 0], ALU.subtract))
                step(dve.tensor_copy(m_parts[:, a, 1], st[:, 5, a]))
                dve.tensor_tensor(m_parts[:, a, 2], st[:, 5, a], m_parts[:, a, 1], ALU.subtract)\
                    .then_inc(S["mcol_ready"], 1)

            def mask_weights(c):
                for g in range(6):
                    v.wait_ge(S["exp_ready"], 8 * c + g + 1)
                    e = attn[:, 2 * g:2 * g + 2, c * CH:(c + 1) * CH]
                    dve.tensor_tensor(e, e, mask8[:, 2 * g:2 * g + 2, c * CH:(c + 1) * CH], ALU.mult)\
                        .then_inc(S["masked_v"], 1)

            def propagated(k, c):
                v.wait_ge(S["prod0_ready"], NC * (k - 1) + c + 1)
                a = slice(TC * c, TC * c + TC)
                width = D + 1 if k == 1 else D
                acc = ps[:, 6 if k == 1 else 7 - c % 2, 0:TC * width].rearrange("p (t f) -> p t f", t=TC)
                if k == 1:
                    step(dve.reciprocal(st[:, 6, a], acc[:, :, D]))
                dve.tensor_tensor(u_buf[(k + 1) % 2][:, a, :], acc[:, :, 0:D],
                                  st[:, 6, a].unsqueeze(2).to_broadcast([P, TC, D]), ALU.mult)\
                    .then_inc(S["prod0_read"], 1)

            for c in range(NC + 2):
                if c < NC:
                    row_max(c)
                if 1 <= c <= NC:
                    mask_weights(c - 1)
                if c >= 2:
                    propagated(1, c - 2)
            for k in (2, 3, 4):
                if k != 4:
                    v.wait_ge(S["prod0_read"], NC * (k - 1))
                    step(dve.scalar_tensor_tensor(xs[:, :, :], u_buf[k % 2], (1.0, 0.5)[k - 2], xs[:, :, :],
                                                  ALU.mult, ALU.add))
                for c in range(NC):
                    propagated(k, c)
            v.wait_ge(S["prod0_read"], 4 * NC)
            step(dve.scalar_tensor_tensor(xs[:, :, :], u_buf[1], 1.0 / 6.0, xs[:, :, :], ALU.mult, ALU.add))

            layer_norm(3)
            step(dve.tensor_scalar(h_feat, xc, 0.0, None, ALU.max))
            step(dve.tensor_tensor(sq, h_feat, h_feat, ALU.mult))
            step(dve.tensor_reduce(stat(5), sq, X, ALU.add))
            dve.tensor_copy(feat[:, :, D + 1], stat(5))
            dve.tensor_scalar(feat_a[:, :, 0:D], h_feat, -2.0, None, ALU.mult)
            dve.tensor_copy(feat_a[:, :, D], stat(5))
            dve.memset(feat_a[:, :, D + 1:D + 2], 1.0)
            dve.tensor_scalar(feat_b[:, :, 0:D], h_feat, -2.0, None, ALU.mult)
            dve.memset(feat_b[:, :, D:D + 1], 1.0)
            dve.tensor_copy(feat_b[:, :, D + 1], stat(5)).then_inc(S["feat_ready"], 1)
            for g in range(NC):
                v.wait_ge(S["t1_ready"], 3 * g + 2)
                dve.tensor_copy(xa[0:AUG, g * CH:(g + 1) * CH], ps[0:AUG, 1, :]).then_inc(S["xa_ready"], 1)

            for c in range(NCH + 3):
                if c < NCH:
                    r = c % 3
                    v.wait_ge(S["gram_ready"], c + 1)
                    step(dve.tensor_scalar(ring["den"][r], ps[:, 2 * (c % 2) + 1, :], EPS1, None, ALU.max))
                    dve.scalar_tensor_tensor(ring["dist"][r], ring["den"][r], UMAX * UMAX, ps[:, 2 * (c % 2), :],
                                             ALU.mult, ALU.min).then_inc(S["gram_read"], 1)
                if 1 <= c <= NCH:
                    b = c - 1
                    v.wait_ge(S["invs_ready"], b + 1)
                    if b >= 3:
                        v.wait_ge(S["ln_ready"], b - 2)
                    dve.scalar_tensor_tensor(ring["un"][b % 3], ring["dist"][b % 3], DMIN, ring["inv_s"][b % 3],
                                             ALU.max, ALU.mult).then_inc(S["un_ready"], 1)
                if c < NCH:
                    v.wait_ge(S["gram_read"], c + 1)
                    dve.scalar_tensor_tensor(ring["prod"][r], ring["dist"][r], DMIN, ring["den"][r],
                                             ALU.max, ALU.mult).then_inc(S["p_ready"], 1)
                if 2 <= c < NCH + 2:
                    b = c - 2
                    v.wait_ge(S["atn_ready"], b + 1)
                    if b >= 3:
                        v.wait_ge(S["wup_ready"], wup_count[b - 2])
                        v.wait_ge(S["wt_ready"], b - 2)
                    dve.tensor_tensor(ring["w"][b % 3], ring["atn"][b % 3], ring["inv_s"][b % 3], ALU.mult)\
                        .then_inc(S["w_ready"], 1)
                if c >= 3:
                    b = c - 3
                    v.wait_ge(S["wt_ready"], b + 1)
                    if b >= 3:
                        v.wait_ge(S["sum1_done"], b - 2)
                    rr = runs(CHUNKS[b], False)
                    for k, (s, n, j, i) in enumerate(rr):
                        last = dve.tensor_tensor(
                            ring["w_lo"][b % 3][:, s * P:(s + n) * P].rearrange("p (t i) -> p t i", t=n),
                            ps[:, 4, s * P:(s + n) * P].rearrange("p (t i) -> p t i", t=n),
                            mask8[:, i:i + n, j * P:(j + 1) * P], ALU.mult)
                    if rr:
                        last.then_inc(S["wlo_ready"], 1)
                    else:
                        v.sem_inc(S["wlo_ready"], 1)

            v.wait_ge(S["sum1_done"], NCH)
            for b in range(3):
                n = min(PER_BANK, T - PER_BANK * b)
                step(dve.tensor_copy(agg[:, PER_BANK * b:PER_BANK * b + n, :],
                                     ps[:, 5 + b, 0:n * AUG].rearrange("p (t f) -> p t f", t=n)))
            step(dve.tensor_tensor(sq, h_feat, agg[:, :, 0:D], ALU.mult))
            step(dve.tensor_reduce(stat(0), sq, X, ALU.add))
            step(dve.tensor_scalar(stat(6), stat(5), -1.0, 1.0, ALU.mult, ALU.add))
            step(dve.tensor_tensor(stat(1), agg[:, :, D], agg[:, :, D + 1], ALU.add))
            step(dve.scalar_tensor_tensor(stat(0), stat(0), -2.0, stat(1), ALU.mult, ALU.add))
            step(dve.tensor_tensor(xc, agg[:, :, 0:D], over_features(stat(6)), ALU.mult))
            step(dve.tensor_tensor(sq, h_feat, over_features(stat(0)), ALU.mult))
            step(dve.tensor_tensor(xc, xc, sq, ALU.subtract))
            step(dve.tensor_scalar(xc, xc, 0.5, None, ALU.mult))
            step(dve.tensor_tensor(sq, xc, xc, ALU.mult))
            step(dve.tensor_reduce(stat(12), sq, X, ALU.add))
            dve.tensor_scalar(stat(7), stat(12), 1e-30, None, ALU.max).then_inc(S["norm_a"], 1)
            step(dve.tensor_tensor(sq, h_feat, xc, ALU.mult))
            step(dve.tensor_reduce(stat(13), sq, X, ALU.add))
            step(dve.tensor_scalar(stat(9), stat(6), EPS1, None, ALU.max))
            step(dve.reciprocal(stat(14), stat(9)))
            v.wait_ge(S["norm_b"], 1)
            step(dve.tensor_tensor(stat(8), stat(8), stat(9), ALU.mult))
            step(dve.tensor_scalar(stat(8), stat(8), EPS1, None, ALU.max))
            dve.tensor_tensor(stat(10), stat(8), stat(14), ALU.mult).then_inc(S["tanh_a"], 1)
            step(dve.reciprocal(stat(15), stat(8)))
            step(dve.tensor_tensor(stat(15), stat(15), stat(9), ALU.mult))
            v.wait_ge(S["tanh_b"], 1)
            step(dve.tensor_tensor(stat(15), stat(15), stat(11), ALU.mult))
            step(dve.tensor_tensor(stat(13), stat(13), stat(15), ALU.mult))
            step(dve.tensor_tensor(stat(16), stat(15), stat(15), ALU.mult))
            step(dve.tensor_tensor(stat(16), stat(16), stat(12), ALU.mult))
            step(dve.tensor_scalar(stat(13), stat(13), 2.0, 1.0, ALU.mult, ALU.add))
            step(dve.tensor_tensor(stat(0), stat(5), stat(16), ALU.mult))
            step(dve.tensor_tensor(stat(0), stat(0), stat(13), ALU.add))
            step(dve.tensor_scalar(stat(0), stat(0), EPS1, None, ALU.max))
            step(dve.reciprocal(stat(1), stat(0)))
            step(dve.tensor_tensor(stat(13), stat(13), stat(16), ALU.add))
            step(dve.tensor_tensor(stat(13), stat(13), stat(1), ALU.mult))
            step(dve.tensor_tensor(stat(6), stat(6), stat(15), ALU.mult))
            step(dve.tensor_tensor(stat(6), stat(6), stat(1), ALU.mult))
            step(dve.tensor_tensor(xc, xc, over_features(stat(6)), ALU.mult))
            step(dve.tensor_tensor(sq, h_feat, over_features(stat(13)), ALU.mult))
            step(dve.tensor_tensor(xc, xc, sq, ALU.add))
            dve.tensor_tensor(xs[:, :, :], xs[:, :, :], xc, ALU.add).then_inc(S["layer1_done"], 1)
            v.wait_ge(S["layer1_done"], 1)

            layer_norm(4)
            dve.tensor_scalar(h_feat, xc, 0.0, None, ALU.max).then_inc(S["feat_ready"], 1)
            v.wait_ge(S["wa_ready"], 1)
            dve.tensor_copy(w2_sb[:, D:D + 2], ps[0:D, 4, 0:2]).then_inc(S["wa_set"], 1)
            v.wait_ge(S["wh_ready"], 1)
            for b in range(3):
                n = min(PER_BANK, T - PER_BANK * b)
                a = slice(PER_BANK * b, PER_BANK * b + n)
                src = ps[:, 5 + b, 0:n * AUG].rearrange("p (t f) -> p t f", t=n)
                dve.tensor_copy(wh[:, a, 0:D], src[:, :, 0:D])
                dve.tensor_copy(st[:, 15, a], src[:, :, D])
                step(dve.tensor_copy(st[:, 16, a], src[:, :, D + 1]))
            dve.memset(wh[:, :, D:D + 1], 1.0)
            step(dve.tensor_scalar(stat(17), stat(16), ALPHA, None, ALU.mult))
            step(dve.tensor_scalar(stat(19), stat(16), 1.0 - ALPHA, None, ALU.mult))
            dve.tensor_reduce(st[:, 18, 0:1], stat(16), X, ALU.min).then_inc(S["min_ready"], 1)
            v.wait_ge(S["min_t"], 1)
            dve.tensor_reduce(st[0:1, 18, 1:2], ps[0:1, 4, 0:P], X, ALU.min).then_inc(S["min_r"], 1)
            v.wait_ge(S["min_b"], 1)
            step(dve.tensor_copy(st[:, 18, 2:3], ps[:, 4, P:P + 1]))
            step(dve.tensor_scalar(stat(22), stat(16), st[:, 18, 2:3], None, ALU.subtract))
            step(dve.tensor_scalar(best, mask8[:, 0, :], st[:, 22, 0:1], None, ALU.mult))
            for j in range(1, T):
                ins = dve.scalar_tensor_tensor(best, mask8[:, j, :], st[:, 22, j:j + 1], best, ALU.mult, ALU.max)
                if j < T - 1:
                    step(ins)
            ins.then_inc(S["best_ready"], 1)
            v.wait_ge(S["bt_ready"], 1)
            step(dve.tensor_reduce(stat(0), ps[:, 0:NC, :].rearrange("p b (k i) -> p (b k) i", k=TC), X, ALU.max))
            step(dve.tensor_scalar(stat(0), stat(0), st[:, 18, 2:3], None, ALU.add))
            step(dve.tensor_tensor(stat(0), stat(0), stat(15), ALU.add))
            step(dve.scalar_tensor_tensor(stat(0), stat(0), ALPHA, stat(0), ALU.mult, ALU.max))
            step(dve.tensor_tensor(stat(20), stat(15), stat(0), ALU.subtract))
            dve.scalar_tensor_tensor(stat(21), stat(15), ALPHA, stat(0), ALU.mult, ALU.subtract)\
                .then_inc(S["m_ready"], 1)
            v.wait_ge(S["rows_ready"], 2)
            dve.tensor_copy(row_2.rearrange("p (b c) -> p b c", b=NC), ps[:, NC:2 * NC, :]).then_inc(S["row1_set"], 1)
            v.wait_ge(S["row1_set"], 2)
            for j in range(T + 1):
                if j < T:
                    if j >= 3:
                        v.wait_ge(S["sum2_done"], j - 2)
                    dve.scalar_tensor_tensor(p_ring[j % 3], row_1, st[:, 19, j:j + 1], row_2, ALU.add, ALU.max)\
                        .then_inc(S["z_ready"], 1)
                if j >= 1:
                    v.wait_ge(S["pe_ready"], j)
                    dve.scalar_tensor_tensor(p_ring[(j - 1) % 3], mask8[:, j - 1, :], 2.0, p_ring[(j - 1) % 3],
                                             ALU.mult, ALU.min).then_inc(S["pm_ready"], 1)
            v.wait_ge(S["sum2_done"], T)
            for b in range(3):
                n = min(PER_BANK, T - PER_BANK * b)
                step(dve.tensor_copy(agg2[:, PER_BANK * b:PER_BANK * b + n, 0:D + 1],
                                     ps[:, 5 + b, 0:n * (D + 1)].rearrange("p (t f) -> p t f", t=n)))
            step(dve.reciprocal(stat(0), agg2[:, :, D]))
            step(dve.tensor_tensor(xc, agg2[:, :, 0:D], over_features(stat(0)), ALU.mult))
            dve.tensor_scalar(sq, xc, 0.0, None, ALU.min).then_inc(S["elu_ready"], 1)
            step(dve.scalar_tensor_tensor(xs[:, :, :], xc, 0.0, xs[:, :, :], ALU.max, ALU.add))
            v.wait_ge(S["elu_exp"], 1)
            step(dve.scalar_tensor_tensor(xs[:, :, :], sq, -1.0, xs[:, :, :], ALU.add, ALU.add))

            layer_norm(5)
            dve.tensor_scalar(h_feat, xc, 0.0, None, ALU.max).then_inc(S["feat_ready"], 1)
            v.wait_ge(S["h3_ready"], 1)
            src = ps[:, 4:8, :].rearrange("p b (k f) -> p (b k) f", k=TC)
            step(dve.tensor_copy(parts3[:, :, 0:D], src[:, :, 0:D]))
            step(dve.tensor_tensor(r3, src[:, :, 0:D], parts3[:, :, 0:D], ALU.subtract))
            step(dve.tensor_copy(parts3[:, :, D:2 * D], r3))
            dve.memset(parts3[:, :, 3 * D:PW], 1.0)
            dve.tensor_tensor(parts3[:, :, 2 * D:3 * D], r3, parts3[:, :, D:2 * D], ALU.subtract)\
                .then_inc(S["parts_ready"], 1)
            step(dve.tensor_tensor(self3, src[:, :, D:2 * D], xs[:, :, :], ALU.add))
            step(dve.tensor_tensor(self3, self3, bias_sb[:, :].unsqueeze(1).to_broadcast([P, T, D]), ALU.add))
            for g in range(T // 2):
                a = slice(2 * g, 2 * g + 2)
                v.wait_ge(S["sum3_ready"], g + 1)
                acc = ps[:, g % 4, 0:2 * PW].rearrange("p (t f) -> p t f", t=2)
                step(dve.reciprocal(st[:, 23, a], acc[:, :, 3 * D]))
                dve.tensor_reduce(r3[:, a, :], acc[:, :, 0:3 * D].rearrange("p t (s f) -> p t f s", s=3), X, ALU.add)\
                    .then_inc(S["sum3_read"], 1)
                v.wait_ge(S["sum3_read"], g + 1)
                step(dve.tensor_tensor(r3[:, a, :], r3[:, a, :], st[:, 23, a].unsqueeze(2).to_broadcast([P, 2, D]),
                                       ALU.mult))
                ins = dve.tensor_tensor(xs[:, a, :], r3[:, a, :], self3[:, a, :], ALU.add)
                if g % 4 == 3:
                    ins.then_inc(S["y_ready"], 1)


def kernel(x, adj, L0_gnn_w_k, L0_gnn_w_q, L2_gnn_W, L2_gnn_a, L3_gnn_weight, L3_gnn_bias):
    import numpy as np
    import concourse.bacc as bacc
    from concourse.bass_utils import run_bass_kernel_spmd as run

    sel = np.zeros((P, 4), np.float32)
    for r in range(KP):
        a, b = r // EMB // 3, r // EMB % 3
        sel[r] = (-(a > 0), -(a > 1), -(b > 0), -(b > 1))
    f = np.asarray
    arrays = {
        "x": np.ascontiguousarray(f(x)),
        "adj_t": np.ascontiguousarray(f(adj).T),
        "w_k": np.ascontiguousarray(f(L0_gnn_w_k)),
        "w_q": np.ascontiguousarray(f(L0_gnn_w_q)),
        "w2": np.ascontiguousarray(f(L2_gnn_W)),
        "w2_t": np.ascontiguousarray(f(L2_gnn_W).T),
        "a2": np.ascontiguousarray(f(L2_gnn_a).reshape(2, D).T),
        "w3": np.ascontiguousarray(f(L3_gnn_weight)),
        "bias3": np.ascontiguousarray(f(L3_gnn_bias)),
        "sel": sel,
        "ident": np.eye(P, dtype=np.float32),
    }
    nc = bacc.Bacc("TRN2", target_bir_lowering=False, num_devices=1)
    args = [nc.dram_tensor("in_" + n, a.shape, mybir.dt.from_np(a.dtype), kind="ExternalInput").ap()
            for n, a in arrays.items()]
    out = nc.dram_tensor("out", (N, D), F32, kind="ExternalOutput").ap()
    build(nc, *args, out)
    r = run(nc, [{"in_" + n: a for n, a in arrays.items()}], core_ids=[0])
    return r.results[0]["out"]
```

```python
from contextlib import ExitStack

import concourse.bass as bass
from concourse import mybir

P = 128
N = 2048
D = 64
T = N // P
EMB = 8
CH = 512
NC = N // CH
TC = CH // P
KP = 9 * EMB
MROW = 96
KM = MROW + 3
AUG = D + 2
PER_BANK = 7
LN_EPS = 1e-5
EPS0 = 1e-12
EPS1 = 1e-7
UMAX = 1.0 - 1e-5
DMIN = 1e-9
ALPHA = 0.2
R = 5

F32 = mybir.dt.float32
BF16 = mybir.dt.bfloat16
F8 = mybir.dt.float8e4
I32 = mybir.dt.int32
ALU = mybir.AluOpType
ACT = mybir.ActivationFunctionType
X = mybir.AxisListType.X

TRI = [(j, i) for j in range(T) for i in range(j, T)]
CHUNKS = [TRI[c:c + TC] for c in range(0, len(TRI), TC)]
NCH = len(CHUNKS)
POOL_J = (3, 7, 11, 15)


def runs(chunk, diagonal):
    out = []
    for s, (j, i) in enumerate(chunk):
        if i == j and not diagonal:
            continue
        if out and out[-1][2] == j and out[-1][0] + out[-1][1] == s:
            out[-1][1] += 1
        else:
            out.append([s, 1, j, i])
    return out


def build(nc, x, adj_t, w_k, w_q, w2, w2_t, a2, w3, bias3, sel, ident, out):
    ctx = ExitStack()
    with ctx:
        def sb(name, shape, dt=F32):
            return ctx.enter_context(nc.sbuf_tensor(name, shape, dt))

        def sem(name):
            return ctx.enter_context(nc.semaphore(name))

        ps = ctx.enter_context(nc.psum_tensor("ps", [P, 8, CH], F32))

        big = sb("big", [P, T * N])
        mask8 = sb("mask8", [P, T, N], F8)
        ht = sb("ht", [P, N])
        scratch = sb("scratch", [P, N])
        k_part = sb("k_part", [P, N], BF16)
        q_part = sb("q_part", [P, N], BF16)
        rounded = sb("rounded", [P, N], BF16)
        xs = sb("xs", [P, T, D])
        feat = sb("feat", [P, T, AUG])
        idf = sb("idf", [P, P])
        idb = sb("idb", [P, P], BF16)
        wk_rep = sb("wk_rep", [D, 9, EMB])
        wq_rep = sb("wq_rep", [D, 9, EMB])
        wkq = sb("wkq", [D, 2, EMB])
        sel_sb = sb("sel_sb", [P, 4])
        w2_sb = sb("w2_sb", [D, AUG])
        w2t_sb = sb("w2t_sb", [D, D])
        a2_sb = sb("a2_sb", [D, 2])
        w3_sb = sb("w3_sb", [D, 2, D])
        bias_sb = sb("bias_sb", [P, D])
        st = sb("st", [P, 24, T])
        rowmax = sb("rowmax", [P, T, 2])
        m_parts = sb("m_parts", [P, T, 3], BF16)
        half_col = sb("half_col", [P, 2])

        attn = big[:, :].rearrange("p (j i) -> p j i", j=T)
        adj_stage = big[:, :].bitcast(I32).rearrange("p (j i) -> p j i", j=T)
        ut_buf = rounded[:, :].bitcast(F32).rearrange("p (b c) -> p b c", b=2)
        u_buf = [ht[:, b * T * D:(b + 1) * T * D].rearrange("p (t f) -> p t f", t=T) for b in range(2)]
        xc = scratch[:, 0:T * D].rearrange("p (t f) -> p t f", t=T)
        sq = scratch[:, T * D:2 * T * D].rearrange("p (t f) -> p t f", t=T)
        h_feat = feat[:, :, 0:D]

        cut = [0]

        def carve(n):
            cut[0] += n
            return big[:, cut[0] - n:cut[0]]
        feat_a = carve(T * AUG).rearrange("p (t f) -> p t f", t=T)
        xt, xa, b_row = carve(N), carve(N), carve(N)
        ring = {n: [carve(CH) for _ in range(R)] for n in
                ("den", "dist", "prod", "inv_s", "atn", "w", "w_up", "w_lo")}
        agg = carve(T * AUG).rearrange("p (t f) -> p t f", t=T)
        assert cut[0] <= T * N
        cut[0] = 0
        row_1, row_2, best = carve(N), carve(N), carve(N)
        p_ring = [carve(N) for _ in range(R)]
        wh = carve(T * AUG).rearrange("p (t f) -> p t f", t=T)
        assert cut[0] <= T * N
        cut[0] = 0
        agg2 = carve(T * AUG).rearrange("p (t f) -> p t f", t=T)
        self3 = carve(T * D).rearrange("p (t f) -> p t f", t=T)
        r3 = carve(T * D).rearrange("p (t f) -> p t f", t=T)
        PW = 3 * D + 1
        parts3 = carve(T * (PW + 1) // 2).bitcast(BF16)[:, 0:T * PW].rearrange("p (t f) -> p t f", t=T)
        assert cut[0] <= 6 * N

        def stat(n):
            return st[:, n, :]

        def over_features(ap, width=D):
            return ap.unsqueeze(2).to_broadcast([P, T, width])

        names = """x_in w_in const_set adj_cast var_ready std_ready feat_ready tr_ready ht_ready
        rep_ready rnd_ready part_ready gmax_ready gmax_read mcol_ready mrow_ready mrow_set score_ready
        exp_ready masked_v masked_g prod0_ready prod0_read ut_ready t0_ready pad_set brow_ready brow_set den_ready
        t1_ready xt_ready xa_ready gram_ready gram_read p_ready invs_ready un_ready ln_ready atn_ready
        w_ready wt_ready wlo_ready wup_ready sum1_done step lift_ready lift2_ready wa_ready wh_ready wh_read ab_ready
        best_ready bt_ready m_ready rows_ready row1_set aggt_ready aggt_set aggt_back z_ready pe_ready pm_ready sum2_done elu_ready
        elu_exp h3_ready h3_read parts_ready sum3_ready sum3_read y_ready out_done
        min_ready min_t min_r min_b norm_a norm_b tanh_a tanh_b wa_set layer1_done zc_ready pg_ready""".split()
        S = {n: sem(n) for n in names}
        adj_in = [sem(f"adj_in_{j}") for j in range(T)]

        block = ctx.enter_context(nc.Block())

        agg_t = scratch[:, :]

        def acc_1(t, width=AUG):
            return ps[:, 5 + t // PER_BANK, (t % PER_BANK) * width:(t % PER_BANK + 1) * width]

        SLOT, ORDER = {}, []

        def plan(kind, c):
            for g in range(8 * c, 8 * c + 8):
                SLOT[kind, g] = len(ORDER) % 3
                ORDER.append((kind, g))
        for c in range(NC + 1):
            if c < NC:
                plan("max", c)
            if c >= 1:
                plan("score", c - 1)

        def bias_one():
            return half_col[0:1, 0:1].to_broadcast([1, P])

        @block.sync
        def _(sp):
            sp.dma_start(xs[:, :, :], x.rearrange("(t p) f -> p t f", p=P)).then_inc(S["x_in"], 16)
            for dst, src in ((idf[:, :], ident), (sel_sb[:, :], sel), (wkq[:, 0, :], w_k), (wkq[:, 1, :], w_q),
                             (w2_sb[:, 0:D], w2), (w2t_sb[:, :], w2_t), (a2_sb[:, :], a2),
                             (w3_sb[:, :, :], w3.rearrange("(s k) f -> k s f", s=2)),
                             (bias_sb[:, :], bias3.partition_broadcast(P))):
                sp.dma_start(dst, src).then_inc(S["w_in"], 16)
            for j in range(T):
                sp.dma_start(adj_stage[:, j, :], adj_t[j * P:(j + 1) * P, :]).then_inc(adj_in[j], 16)
            for h in range(2):
                sp.wait_ge(S["y_ready"], h + 1)
                sp.dma_start(out.rearrange("(t p) f -> p t f", p=P)[:, h * 8:h * 8 + 8, :],
                             xs[:, h * 8:h * 8 + 8, :]).then_inc(S["out_done"], 16)
            sp.wait_ge(S["out_done"], 32)

        W_IN = 16 * 9

        @block.gpsimd
        def _(pool):
            nc.gpsimd.memset(k_part[:, :], 0.0).then_inc(S["const_set"], 1)
            nc.gpsimd.memset(q_part[:, :], 0.0).then_inc(S["const_set"], 1)
            nc.gpsimd.memset(feat[:, :, D:D + 1], 1.0).then_inc(S["const_set"], 1)
            nc.gpsimd.memset(half_col[:, :], 1.0).then_inc(S["const_set"], 1)
            pool.wait_ge(S["const_set"], 4)
            nc.gpsimd.memset(q_part[MROW:KM, :], -1.0).then_inc(S["const_set"], 1)
            pool.wait_ge(S["const_set"], 5)
            for j in range(T):
                pool.wait_ge(adj_in[j], 16)
                nc.gpsimd.tensor_copy(mask8[:, j, :], adj_stage[:, j, :], saturate=False)\
                    .then_inc(S["adj_cast"], 1)
            for c in range(NC):
                for g in (6, 7):
                    pool.wait_ge(S["exp_ready"], 8 * c + g + 1)
                    e = attn[:, 2 * g:2 * g + 2, c * CH:(c + 1) * CH]
                    nc.gpsimd.tensor_tensor(e, e, mask8[:, 2 * g:2 * g + 2, c * CH:(c + 1) * CH],
                                            ALU.mult).then_inc(S["masked_g"], 1)
            pool.wait_ge(S["prod0_ready"], NC + 6)
            for m in (xt, xa):
                nc.gpsimd.memset(m[D:P, :], 0.0).then_inc(S["pad_set"], 1)
            pool.wait_ge(S["pad_set"], 2)
            for c in range(NCH + 3):
                if c < NCH:
                    pool.wait_ge(S["invs_ready"], c + 1)
                    nc.gpsimd.tensor_tensor(ring["dist"][c % R], ring["dist"][c % R], ring["inv_s"][c % R],
                                            ALU.mult).then_inc(S["un_ready"], 1)
                if 1 <= c <= NCH:
                    b = c - 1
                    pool.wait_ge(S["ln_ready"], b + 1)
                    nc.gpsimd.tensor_tensor(ring["atn"][b % R], ring["atn"][b % R], ring["dist"][b % R],
                                            ALU.subtract).then_inc(S["atn_ready"], 1)
                if c >= 3:
                    b = c - 3
                    pool.wait_ge(S["w_ready"], b + 1)
                    if b >= R:
                        pool.wait_ge(S["sum1_done"], b - R + 1)
                    for s, n, j, i in runs(CHUNKS[b], True):
                        nc.gpsimd.tensor_tensor(ring["w_up"][b % R][:, s * P:(s + n) * P],
                                                ring["w"][b % R][:, s * P:(s + n) * P],
                                                mask8[:, j, i * P:(i + n) * P], ALU.mult).then_inc(S["wup_ready"], 1)
            for n, j in enumerate(POOL_J):
                pool.wait_ge(S["z_ready"], j + 1)
                nc.gpsimd.tensor_scalar(p_ring[j % R], p_ring[j % R], st[:, 13, j:j + 1], None,
                                        ALU.min).then_inc(S["zc_ready"], 1)
                pool.wait_ge(S["pe_ready"], j + 1)
                nc.gpsimd.tensor_tensor(p_ring[j % R], p_ring[j % R], mask8[:, j, :], ALU.mult)\
                    .then_inc(S["pg_ready"], 1)

        wup_count = [0]
        for ch in CHUNKS:
            wup_count.append(wup_count[-1] + len(runs(ch, True)))

        @block.scalar
        def _(act):
            def root(ready, value, dst, src, done):
                act.wait_ge(S[ready], value)
                nc.scalar.activation(dst, src, ACT.Sqrt).then_inc(S[done], 1)

            def transposed(tr0):
                for g in range(NC):
                    act.wait_ge(S["tr_ready"], tr0 + g + 1)
                    nc.scalar.copy(ht[0:D, g * CH:(g + 1) * CH], ps[0:D, g, :]).then_inc(S["ht_ready"], 1)

            root("var_ready", 1, stat(3), stat(2), "std_ready")
            root("var_ready", 2, stat(3), stat(2), "std_ready")
            transposed(0)
            for n in range(2):
                act.wait_ge(S["rep_ready"], n + 1)
                if n:
                    act.wait_ge(S["part_ready"], 2)
                nc.scalar.copy(rounded[0:KP, :].rearrange("p (b c) -> p b c", b=NC),
                               ps[0:KP, 4 * n:4 * n + 4, :]).then_inc(S["rnd_ready"], 1)
                act.wait_ge(S["part_ready"], 2 * n + 1)
                nc.scalar.copy(rounded[0:KP, :], scratch[0:KP, :]).then_inc(S["rnd_ready"], 1)
            def u1_copy(c):
                act.wait_ge(S["prod0_ready"], c + 1)
                if c >= 2:
                    act.wait_ge(S["t0_ready"], c - 1)
                nc.scalar.copy(ut_buf[0:D + 1, c % 2, :], ps[0:D + 1, 6, :]).then_inc(S["ut_ready"], 1)

            for c in range(NC):
                if c >= 2:
                    u1_copy(c - 2)
                act.wait_ge(S["mrow_ready"], c + 1)
                nc.scalar.copy(k_part[MROW:KM, c * CH:(c + 1) * CH], ps[MROW:KM, 7, :]).then_inc(S["mrow_set"], 1)
                for g in range(8):
                    act.wait_ge(S["score_ready"], 8 * c + g + 1)
                    if c == 0:
                        act.wait_ge(S["adj_cast"], 2 * g + 2)
                    b = 2 * SLOT["score", 8 * c + g]
                    nc.scalar.activation(attn[:, 2 * g:2 * g + 2, c * CH:(c + 1) * CH], ps[:, b:b + 2, :],
                                         ACT.Exp, scale=EMB ** -0.5).then_inc(S["exp_ready"], 1)
            for c in (NC - 2, NC - 1):
                u1_copy(c)
            for n in range(6):
                act.wait_ge(S["prod0_ready"], NC + n + 1)
                act.wait_ge(S["t0_ready"], NC + n - 1)
                nc.scalar.copy(ut_buf[:, n % 2, :], ps[:, n % 2, :]).then_inc(S["ut_ready"], 1)
            root("var_ready", 3, stat(3), stat(2), "std_ready")
            nc.scalar.preload_act_table_set("natural_log_exp_and_others")
            act.wait_ge(S["pad_set"], 2)
            for g in range(NC):
                act.wait_ge(S["t1_ready"], 2 * g + 1)
                nc.scalar.copy(xt[0:AUG, g * CH:(g + 1) * CH], ps[0:AUG, 0, :]).then_inc(S["xt_ready"], 1)
            act.wait_ge(S["brow_ready"], 1)
            nc.scalar.copy(b_row.rearrange("p (b c) -> p b c", b=NC), ps[:, 4:8, :]).then_inc(S["brow_set"], 1)
            for c in range(NCH + 1):
                if c < NCH:
                    act.wait_ge(S["p_ready"], c + 1)
                    nc.scalar.activation(ring["prod"][c % R], ring["prod"][c % R], ACT.Ln,
                                         scale=1.0 / UMAX ** 2).then_inc(S["lift_ready"], 1)
                    act.wait_ge(S["lift_ready"], c + 1)
                    if c >= R:
                        act.wait_ge(S["w_ready"], c - R + 1)
                    nc.scalar.activation(ring["inv_s"][c % R], ring["prod"][c % R], ACT.Exp,
                                         scale=-0.5).then_inc(S["invs_ready"], 1)
                if c >= 1:
                    b = c - 1
                    act.wait_ge(S["un_ready"], b + 1)
                    nc.scalar.activation(ring["atn"][b % R], ring["dist"][b % R], ACT.Ln, bias=half_col[:, 1:2])\
                        .then_inc(S["lift2_ready"], 1)
                    act.wait_ge(S["lift2_ready"], b + 1)
                    nc.scalar.activation(ring["dist"][b % R], ring["dist"][b % R], ACT.Ln, bias=half_col[:, 1:2],
                                         scale=-1.0).then_inc(S["ln_ready"], 1)
            act.wait_ge(S["sum1_done"], NCH)
            nc.scalar.copy(agg_t[0:AUG, :].rearrange("p (b c) -> p b c", b=NC), ps[0:AUG, 4:8, :])\
                .then_inc(S["aggt_ready"], 1)
            root("norm_a", 1, stat(8), stat(7), "norm_b")
            act.wait_ge(S["tanh_a"], 1)
            nc.scalar.activation(stat(11), stat(10), ACT.Tanh).then_inc(S["tanh_b"], 1)
            root("var_ready", 4, stat(3), stat(2), "std_ready")
            transposed(4)
            act.wait_ge(S["rows_ready"], 1)
            nc.scalar.copy(row_1.rearrange("p (b c) -> p b c", b=NC), ps[:, 0:NC, :]).then_inc(S["row1_set"], 1)
            for j in range(T):
                if j in POOL_J:
                    act.wait_ge(S["zc_ready"], POOL_J.index(j) + 1)
                else:
                    act.wait_ge(S["z_ready"], j + 1)
                nc.scalar.activation(p_ring[j % R], p_ring[j % R], ACT.Exp,
                                     bias=st[:, 17, j:j + 1]).then_inc(S["pe_ready"], 1)
            act.wait_ge(S["sum2_done"], T)
            nc.scalar.copy(agg_t[0:D + 1, :].rearrange("p (b c) -> p b c", b=NC), ps[0:D + 1, 4:8, :])\
                .then_inc(S["aggt_ready"], 1)
            act.wait_ge(S["elu_ready"], 1)
            nc.scalar.activation(sq, sq, ACT.Exp).then_inc(S["elu_exp"], 1)
            root("var_ready", 5, stat(3), stat(2), "std_ready")
            transposed(8)

        @block.tensor
        def _(pe):
            def transposes(src, g, bank, width):
                for k in range(TC):
                    last = nc.tensor.transpose(ps[0:width, bank, k * P:(k + 1) * P], src[:, TC * g + k, :], idf[:, :])
                return last

            pe.wait_ge(S["w_in"], W_IN)
            pe.wait_ge(S["feat_ready"], 1)
            for g in range(NC):
                transposes(h_feat, g, g, D).then_inc(S["tr_ready"], 1)
            pe.wait_ge(S["wa_set"], 1)
            for n, w in enumerate((wk_rep, wq_rep)):
                for g in range(NC):
                    pe.wait_ge(S["ht_ready"], g + 1 if n else NC)
                    last = nc.tensor.matmul(ps[0:KP, 4 * n + g, :], w[:, :, :], ht[0:D, g * CH:(g + 1) * CH],
                                            start=True, stop=True)
                last.then_inc(S["rep_ready"], 1)
            pe.wait_ge(S["part_ready"], 4)

            def group(kind, n):
                at = ORDER.index((kind, n))
                if at >= 3:
                    k, m = ORDER[at - 3]
                    pe.wait_ge(S["gmax_read" if k == "max" else "exp_ready"], m + 1)
                b = 2 * SLOT[kind, n]
                for h in range(2):
                    if kind == "max":
                        t, q = n // 2, 2 * (n % 2) + h
                        last = nc.tensor.matmul(ps[:, b + h, :], k_part[0:KP, t * P:(t + 1) * P],
                                                q_part[0:KP, q * CH:(q + 1) * CH], start=True, stop=True)
                    else:
                        c, j = n // 8, 2 * (n % 8) + h
                        last = nc.tensor.matmul(ps[:, b + h, :], q_part[0:KM, j * P:(j + 1) * P],
                                                k_part[0:KM, c * CH:(c + 1) * CH], start=True, stop=True)
                last.then_inc(S["gmax_ready" if kind == "max" else "score_ready"], 1)

            def sum_ones(c):
                if c:
                    pe.wait_ge(S["ut_ready"], c)
                pe.wait_ge(S["masked_v"], 6 * (c + 1))
                pe.wait_ge(S["masked_g"], 2 * (c + 1))
                for j in range(T):
                    last = nc.tensor.matmul(ps[0:D + 1, 6, :], feat[:, j, 0:D + 1], attn[:, j, c * CH:(c + 1) * CH],
                                            start=(j == 0), stop=(j == T - 1))
                last.then_inc(S["prod0_ready"], 1)

            def turn_ones(c):
                pe.wait_ge(S["ut_ready"], c + 1)
                pe.wait_ge(S["mrow_set"], min(c + 2, NC))
                if c:
                    pe.wait_ge(S["prod0_read"], c)
                for k in range(TC):
                    last = nc.tensor.transpose(ps[:, 7, k * (D + 1):(k + 1) * (D + 1)],
                                               ut_buf[0:D + 1, c % 2, k * P:(k + 1) * P], idf[0:D + 1, 0:D + 1])
                last.then_inc(S["t0_ready"], 1)

            def turn_pair(n):
                pe.wait_ge(S["ut_ready"], NC + n + 1)
                if n >= 2:
                    pe.wait_ge(S["prod0_read"], NC + n - 1)
                for k in range(TC):
                    last = nc.tensor.transpose(ps[:, 2 + n % 2, k * P:(k + 1) * P],
                                               ut_buf[:, n % 2, k * P:(k + 1) * P], idf[:, :])
                last.then_inc(S["t0_ready"], 1)

            for c in range(NC + 2):
                if c >= 3:
                    turn_ones(c - 3)
                if c < NC:
                    for g in range(8 * c, 8 * c + 8):
                        group("max", g)
                if 1 <= c <= NC:
                    pe.wait_ge(S["mcol_ready"], c)
                    if c > 1:
                        pe.wait_ge(S["mrow_set"], c - 1)
                    if c >= 3:
                        pe.wait_ge(S["prod0_read"], c - 2)
                    for k in range(TC):
                        last = nc.tensor.matmul(ps[MROW:KM, 7, k * P:(k + 1) * P], m_parts[:, TC * (c - 1) + k, :],
                                                idb[:, :], start=True, stop=True)
                    last.then_inc(S["mrow_ready"], 1)
                    pe.wait_ge(S["mrow_set"], c)
                    for g in range(8 * c - 8, 8 * c):
                        group("score", g)
                if c >= 2:
                    sum_ones(c - 2)
            for n in range(6):
                k, pair = 2 + n // 2, n % 2
                for j in range(T):
                    if n == 0:
                        if j == 4:
                            turn_ones(NC - 1)
                        if j % TC == 0:
                            pe.wait_ge(S["prod0_read"], j // TC + 1)
                    else:
                        if j == 4:
                            turn_pair(n - 1)
                        if pair == 0 and j % 8 == 0:
                            pe.wait_ge(S["prod0_read"], NC + n - 2 + j // 8 + 1)
                    for h in range(2):
                        c = 2 * pair + h
                        last = nc.tensor.matmul(ps[h * D:(h + 1) * D, n % 2, :], u_buf[k % 2][:, j, :],
                                                attn[:, j, c * CH:(c + 1) * CH], start=(j == 0), stop=(j == T - 1))
                last.then_inc(S["prod0_ready"], 1)
            turn_pair(5)

            pe.wait_ge(S["feat_ready"], 2)
            pe.wait_ge(S["prod0_read"], NC + 6)
            for g in range(NC):
                for n, src in enumerate((feat, feat_a)):
                    if g:
                        pe.wait_ge(S["xa_ready"] if n else S["xt_ready"], g)
                    transposes(src, g, n, AUG).then_inc(S["t1_ready"], 1)
            for t in range(T):
                last = nc.tensor.matmul(ps[:, 4 + t // TC, (t % TC) * P:(t % TC + 1) * P],
                                        st[:, 6, t:t + 1].to_broadcast([P, P]), idf[:, :], start=True, stop=True)
            last.then_inc(S["brow_ready"], 1)
            pe.wait_ge(S["xt_ready"], NC)
            pe.wait_ge(S["xa_ready"], NC)
            pe.wait_ge(S["brow_set"], 1)

            def gram(c):
                if c >= 2:
                    pe.wait_ge(S["gram_read"], c - 1)
                for s, k, j, i in runs(CHUNKS[c], True):
                    last = nc.tensor.matmul(ps[:, c % 2, s * P:(s + k) * P], xa[:, j * P:(j + 1) * P],
                                            xt[:, i * P:(i + k) * P], start=True, stop=True)
                last.then_inc(S["gram_ready"], 1)

            opened = set()

            def add_to(i, k, src, w):
                bank = 4 + i // TC
                first = bank not in opened
                opened.add(bank)
                return nc.tensor.matmul(ps[0:AUG, bank, (i % TC) * P:(i % TC + k) * P], src, w,
                                        start=first, stop=True, skip_group_check=True)

            for c in range(NCH + 4):
                if c == 0:
                    gram(0)
                if c + 1 < NCH:
                    gram(c + 1)
                if 3 <= c < NCH + 3:
                    b = c - 3
                    pe.wait_ge(S["w_ready"], b + 1)
                    if b >= 2:
                        pe.wait_ge(S["wlo_ready"], b - 1)
                    last = None
                    for s, (j, i) in enumerate(CHUNKS[b]):
                        if i != j:
                            last = nc.tensor.transpose(ps[:, 2 + b % 2, s * P:(s + 1) * P],
                                                       ring["w"][b % R][:, s * P:(s + 1) * P], idf[:, :])
                    if last is None:
                        pe.sem_inc(S["wt_ready"], 1)
                    else:
                        last.then_inc(S["wt_ready"], 1)
                if c >= 4:
                    b = c - 4
                    pe.wait_ge(S["wup_ready"], wup_count[b + 1])
                    for s, k, j, i in runs(CHUNKS[b], True):
                        while k:
                            m = min(k, TC - i % TC)
                            last = add_to(i, m, feat[:, j, :], ring["w_up"][b % R][:, s * P:(s + m) * P])
                            s, k, i = s + m, k - m, i + m
                    pe.wait_ge(S["wlo_ready"], b + 1)
                    for s, (j, i) in enumerate(CHUNKS[b]):
                        if i != j:
                            last = add_to(j, 1, feat[:, i, :], ring["w_lo"][b % R][:, s * P:(s + 1) * P])
                    last.then_inc(S["sum1_done"], 1)

            def turn_sums(n, width):
                pe.wait_ge(S["aggt_ready"], n)
                for t in range(T):
                    last = nc.tensor.transpose(ps[:, t // PER_BANK, (t % PER_BANK) * width:(t % PER_BANK + 1) * width],
                                               agg_t[0:width, t * P:(t + 1) * P], idf[0:width, 0:width])
                last.then_inc(S["aggt_back"], 1)

            turn_sums(1, AUG)

            nc.tensor.matmul(ps[0:D, 4, 0:2], w2t_sb[:, :], a2_sb[:, :], start=True, stop=True)\
                .then_inc(S["wa_ready"], 1)
            pe.wait_ge(S["feat_ready"], 3)
            for g in range(NC):
                transposes(h_feat, g, g, D).then_inc(S["tr_ready"], 1)
            pe.wait_ge(S["wa_set"], 2)
            for g in range(NC):
                pe.wait_ge(S["ht_ready"], NC + g + 1)
                for k in range(TC):
                    t = TC * g + k
                    last = nc.tensor.matmul(acc_1(t), ht[0:D, t * P:(t + 1) * P], w2_sb[:, :],
                                            start=True, stop=True)
            last.then_inc(S["wh_ready"], 1)
            pe.wait_ge(S["min_ready"], 1)
            nc.tensor.transpose(ps[0:1, 4, 0:P], stat(18)[:, 0:1], idf[:, :]).then_inc(S["min_t"], 1)
            pe.wait_ge(S["min_r"], 1)
            nc.tensor.matmul(ps[:, 4, P:P + 1], bias_one(), st[0:1, 18, 1:2], start=True, stop=True)\
                .then_inc(S["min_b"], 1)
            pe.wait_ge(S["best_ready"], 1)
            for t in range(T):
                last = nc.tensor.transpose(ps[:, t // TC, (t % TC) * P:(t % TC + 1) * P],
                                           best[:, t * P:(t + 1) * P], idf[:, :])
            last.then_inc(S["bt_ready"], 1)
            pe.wait_ge(S["m_ready"], 1)
            for n in range(2):
                for t in range(T):
                    last = nc.tensor.matmul(ps[:, 4 * n + t // TC, (t % TC) * P:(t % TC + 1) * P],
                                            st[:, 20 + n, t:t + 1].to_broadcast([P, P]), idf[:, :],
                                            start=True, stop=True)
                last.then_inc(S["rows_ready"], 1)
            pe.wait_ge(S["row1_set"], 2)
            for j in range(T):
                if j in POOL_J:
                    pe.wait_ge(S["pg_ready"], POOL_J.index(j) + 1)
                else:
                    pe.wait_ge(S["pm_ready"], j + 1 - sum(k < j for k in POOL_J))
                for c in range(NC):
                    last = nc.tensor.matmul(ps[0:D + 1, 4 + c, :], wh[:, j, 0:D + 1],
                                            p_ring[j % R][:, c * CH:(c + 1) * CH], start=(j == 0), stop=(j == T - 1))
                last.then_inc(S["sum2_done"], 1)
            turn_sums(2, D + 1)

            pe.wait_ge(S["feat_ready"], 4)
            for g in range(NC):
                transposes(h_feat, g, g, D).then_inc(S["tr_ready"], 1)
            for g in range(NC):
                pe.wait_ge(S["ht_ready"], 2 * NC + g + 1)
                for k in range(TC):
                    t = TC * g + k
                    last = nc.tensor.matmul(ps[:, 4 + g, k * P:(k + 1) * P], ht[0:D, t * P:(t + 1) * P],
                                            w3_sb[:, :, :], start=True, stop=True)
            last.then_inc(S["h3_ready"], 1)
            pe.wait_ge(S["parts_ready"], 1)
            for g in range(T // 2):
                if g >= 4:
                    pe.wait_ge(S["sum3_read"], g - 3)
                for h in range(2):
                    t = 2 * g + h
                    for j in range(T):
                        last = nc.tensor.matmul(ps[:, g % 4, h * PW:(h + 1) * PW], mask8[:, j, t * P:(t + 1) * P],
                                                parts3[:, j, :], start=(j == 0), stop=(j == T - 1))
                last.then_inc(S["sum3_ready"], 1)

        @block.vector
        def _(v):
            dve = nc.vector
            done = [0]

            def step(ins):
                done[0] += 1
                ins.then_inc(S["step"], 1)
                v.wait_ge(S["step"], done[0])

            def centre(src):
                step(dve.tensor_reduce(stat(0), src, X, ALU.add))
                step(dve.tensor_scalar(stat(1), stat(0), -1.0 / D, None, ALU.mult))
                step(dve.tensor_tensor(xc, src, over_features(stat(1)), ALU.add))
                step(dve.tensor_tensor(sq, xc, xc, ALU.mult))
                step(dve.tensor_reduce(stat(0), sq, X, ALU.add))

            def layer_norm(n):
                centre(xs[:, :, :])
                dve.tensor_scalar(stat(2), stat(0), 1.0 / D, LN_EPS, ALU.mult, ALU.add).then_inc(S["var_ready"], 1)
                v.wait_ge(S["std_ready"], n)
                step(dve.reciprocal(stat(4), stat(3)))
                step(dve.tensor_tensor(xc, xc, over_features(stat(4)), ALU.mult))

            v.wait_ge(S["w_in"], W_IN)
            v.wait_ge(S["const_set"], 5)
            step(dve.tensor_copy(wk_rep[:, :, :], wkq[:, 0:1, :].to_broadcast([D, 9, EMB])))
            step(dve.tensor_copy(idb[:, :], idf[:, :]))
            dve.tensor_copy(wq_rep[:, :, :], wkq[:, 1:2, :].to_broadcast([D, 9, EMB])).then_inc(S["wa_set"], 1)
            v.wait_ge(S["x_in"], 16)
            layer_norm(1)
            step(dve.tensor_scalar(h_feat, xc, 0.0, None, ALU.max))
            centre(h_feat)
            dve.tensor_scalar(stat(2), stat(0), EPS0 * EPS0, None, ALU.max).then_inc(S["var_ready"], 1)
            v.wait_ge(S["std_ready"], 2)
            step(dve.reciprocal(stat(4), stat(3)))
            dve.tensor_tensor(h_feat, xc, over_features(stat(4)), ALU.mult).then_inc(S["feat_ready"], 1)
            v.wait_ge(S["feat_ready"], 1)
            for n, part in enumerate((k_part, q_part)):
                v.wait_ge(S["rnd_ready"], 2 * n + 1)
                dve.scalar_tensor_tensor(scratch[0:KP, :].rearrange("p (b c) -> p b c", b=NC),
                                         rounded[0:KP, :].rearrange("p (b c) -> p b c", b=NC),
                                         sel_sb[0:KP, 2 * n:2 * n + 1], ps[0:KP, 4 * n:4 * n + 4, :],
                                         ALU.mult, ALU.add).then_inc(S["part_ready"], 1)
                v.wait_ge(S["rnd_ready"], 2 * n + 2)
                dve.scalar_tensor_tensor(part[0:KP, :], rounded[0:KP, :], sel_sb[0:KP, 2 * n + 1:2 * n + 2],
                                         scratch[0:KP, :], ALU.mult, ALU.add).then_inc(S["part_ready"], 1)

            def row_max(c):
                for g in range(8 * c, 8 * c + 8):
                    v.wait_ge(S["gmax_ready"], g + 1)
                    b = 2 * SLOT["max", g]
                    dve.tensor_reduce(rowmax[:, g // 2, g % 2:g % 2 + 1], ps[:, b:b + 2, :],
                                      mybir.AxisListType.XY, ALU.max).then_inc(S["gmax_read"], 1)
                v.wait_ge(S["gmax_read"], 8 * c + 8)
                a = slice(TC * c, TC * c + TC)
                step(dve.tensor_reduce(st[:, 5, a], rowmax[:, a, :], X, ALU.max))
                step(dve.tensor_copy(m_parts[:, a, 0], st[:, 5, a]))
                step(dve.tensor_tensor(st[:, 5, a], st[:, 5, a], m_parts[:, a, 0], ALU.subtract))
                step(dve.tensor_copy(m_parts[:, a, 1], st[:, 5, a]))
                dve.tensor_tensor(m_parts[:, a, 2], st[:, 5, a], m_parts[:, a, 1], ALU.subtract)\
                    .then_inc(S["mcol_ready"], 1)

            def mask_weights(c):
                for g in range(6):
                    v.wait_ge(S["exp_ready"], 8 * c + g + 1)
                    e = attn[:, 2 * g:2 * g + 2, c * CH:(c + 1) * CH]
                    dve.tensor_tensor(e, e, mask8[:, 2 * g:2 * g + 2, c * CH:(c + 1) * CH], ALU.mult)\
                        .then_inc(S["masked_v"], 1)

            def ones_turned(c):
                v.wait_ge(S["t0_ready"], c + 1)
                a = slice(TC * c, TC * c + TC)
                acc = ps[:, 7, 0:TC * (D + 1)].rearrange("p (t f) -> p t f", t=TC)
                step(dve.reciprocal(st[:, 6, a], acc[:, :, D]))
                dve.tensor_tensor(u_buf[0][:, a, :], acc[:, :, 0:D],
                                  st[:, 6, a].unsqueeze(2).to_broadcast([P, TC, D]), ALU.mult)\
                    .then_inc(S["prod0_read"], 1)

            def pair_turned(n):
                v.wait_ge(S["t0_ready"], NC + n + 1)
                a = slice(8 * (n % 2), 8 * (n % 2) + 8)
                dve.tensor_tensor(u_buf[(n // 2 + 1) % 2][:, a, :].rearrange("p (h k) f -> p k h f", h=2),
                                  ps[:, 2 + n % 2, :].rearrange("p (k h f) -> p k h f", k=TC, h=2),
                                  st[:, 6, a].rearrange("p (h k) -> p k h", h=2).unsqueeze(3)
                                  .to_broadcast([P, TC, 2, D]), ALU.mult).then_inc(S["prod0_read"], 1)

            def add_u(k, factor):
                step(dve.scalar_tensor_tensor(xs[:, :, :], u_buf[(k + 1) % 2], factor, xs[:, :, :],
                                              ALU.mult, ALU.add))

            for c in range(NC + 1):
                if c < NC:
                    row_max(c)
                if c >= 3:
                    ones_turned(c - 3)
                if c >= 1:
                    mask_weights(c - 1)
            ones_turned(NC - 2)
            ones_turned(NC - 1)
            v.wait_ge(S["prod0_read"], NC)
            add_u(1, 1.0)
            for n in range(6):
                pair_turned(n)
                if n == 1:
                    v.wait_ge(S["prod0_read"], NC + 2)
                    add_u(2, 0.5)
            v.wait_ge(S["prod0_read"], NC + 6)
            add_u(4, 1.0 / 6.0)

            layer_norm(3)
            step(dve.tensor_scalar(h_feat, xc, 0.0, None, ALU.max))
            step(dve.tensor_tensor(sq, h_feat, h_feat, ALU.mult))
            step(dve.tensor_reduce(stat(5), sq, X, ALU.add))
            step(dve.tensor_scalar(stat(6), stat(5), -1.0, 1.0, ALU.mult, ALU.add))
            dve.tensor_copy(feat[:, :, D + 1], stat(5))
            dve.tensor_scalar(feat_a[:, :, 0:D], h_feat, -2.0, None, ALU.mult)
            dve.tensor_copy(feat_a[:, :, D], stat(5))
            dve.memset(feat_a[:, :, D + 1:D + 2], 1.0).then_inc(S["feat_ready"], 1)
            v.wait_ge(S["pad_set"], 2)
            for g in range(NC):
                v.wait_ge(S["t1_ready"], 2 * g + 2)
                dve.tensor_copy(xa[0:AUG, g * CH:(g + 1) * CH], ps[0:AUG, 1, :]).then_inc(S["xa_ready"], 1)
            v.wait_ge(S["brow_set"], 1)

            for c in range(NCH + 4):
                if c < NCH:
                    r = c % R
                    v.wait_ge(S["gram_ready"], c + 1)
                    for s, n, j, i in runs(CHUNKS[c], True):
                        last = dve.scalar_tensor_tensor(ring["den"][r][:, s * P:(s + n) * P], b_row[:, i * P:(i + n) * P],
                                                        st[:, 6, j:j + 1], ps[:, c % 2, s * P:(s + n) * P],
                                                        ALU.mult, ALU.add)
                    step(last)
                    step(dve.tensor_scalar(ring["den"][r], ring["den"][r], EPS1, UMAX * UMAX, ALU.max, ALU.mult))
                    dve.scalar_tensor_tensor(ring["dist"][r], ps[:, c % 2, :], DMIN, ring["den"][r],
                                             ALU.max, ALU.min).then_inc(S["gram_read"], 1)
                if 3 <= c < NCH + 3:
                    b = c - 3
                    v.wait_ge(S["atn_ready"], b + 1)
                    if b >= R:
                        v.wait_ge(S["wup_ready"], wup_count[b - R + 1])
                        v.wait_ge(S["wt_ready"], b - R + 1)
                    dve.tensor_tensor(ring["w"][b % R], ring["atn"][b % R], ring["inv_s"][b % R], ALU.mult)\
                        .then_inc(S["w_ready"], 1)
                if c < NCH:
                    v.wait_ge(S["gram_read"], c + 1)
                    dve.tensor_tensor(ring["prod"][r], ring["dist"][r], ring["den"][r], ALU.mult)\
                        .then_inc(S["p_ready"], 1)
                if c >= 4:
                    b = c - 4
                    v.wait_ge(S["wt_ready"], b + 1)
                    if b >= R:
                        v.wait_ge(S["sum1_done"], b - R + 1)
                    rr = runs(CHUNKS[b], False)
                    for k, (s, n, j, i) in enumerate(rr):
                        last = dve.tensor_tensor(
                            ring["w_lo"][b % R][:, s * P:(s + n) * P].rearrange("p (t i) -> p t i", t=n),
                            ps[:, 2 + b % 2, s * P:(s + n) * P].rearrange("p (t i) -> p t i", t=n),
                            mask8[:, i:i + n, j * P:(j + 1) * P], ALU.mult)
                    if rr:
                        last.then_inc(S["wlo_ready"], 1)
                    else:
                        v.sem_inc(S["wlo_ready"], 1)

            def sums_turned(k, dst, width):
                v.wait_ge(S["aggt_back"], k)
                for b in range(3):
                    n = min(PER_BANK, T - PER_BANK * b)
                    step(dve.tensor_copy(dst[:, PER_BANK * b:PER_BANK * b + n, 0:width],
                                         ps[:, b, 0:n * width].rearrange("p (t f) -> p t f", t=n)))

            sums_turned(1, agg, AUG)
            step(dve.tensor_tensor(sq, h_feat, agg[:, :, 0:D], ALU.mult))
            step(dve.tensor_reduce(stat(0), sq, X, ALU.add))
            step(dve.tensor_tensor(stat(1), agg[:, :, D], agg[:, :, D + 1], ALU.add))
            step(dve.scalar_tensor_tensor(stat(0), stat(0), -2.0, stat(1), ALU.mult, ALU.add))
            step(dve.tensor_tensor(xc, agg[:, :, 0:D], over_features(stat(6)), ALU.mult))
            step(dve.tensor_tensor(sq, h_feat, over_features(stat(0)), ALU.mult))
            step(dve.tensor_tensor(xc, xc, sq, ALU.subtract))
            step(dve.tensor_scalar(xc, xc, 0.5, None, ALU.mult))
            step(dve.tensor_tensor(sq, xc, xc, ALU.mult))
            step(dve.tensor_reduce(stat(12), sq, X, ALU.add))
            dve.tensor_scalar(stat(7), stat(12), 1e-30, None, ALU.max).then_inc(S["norm_a"], 1)
            step(dve.tensor_tensor(sq, h_feat, xc, ALU.mult))
            step(dve.tensor_reduce(stat(13), sq, X, ALU.add))
            step(dve.tensor_scalar(stat(9), stat(6), EPS1, None, ALU.max))
            step(dve.reciprocal(stat(14), stat(9)))
            v.wait_ge(S["norm_b"], 1)
            step(dve.tensor_tensor(stat(8), stat(8), stat(9), ALU.mult))
            step(dve.tensor_scalar(stat(8), stat(8), EPS1, None, ALU.max))
            dve.tensor_tensor(stat(10), stat(8), stat(14), ALU.mult).then_inc(S["tanh_a"], 1)
            step(dve.reciprocal(stat(15), stat(8)))
            step(dve.tensor_tensor(stat(15), stat(15), stat(9), ALU.mult))
            v.wait_ge(S["tanh_b"], 1)
            step(dve.tensor_tensor(stat(15), stat(15), stat(11), ALU.mult))
            step(dve.tensor_tensor(stat(13), stat(13), stat(15), ALU.mult))
            step(dve.tensor_tensor(stat(16), stat(15), stat(15), ALU.mult))
            step(dve.tensor_tensor(stat(16), stat(16), stat(12), ALU.mult))
            step(dve.tensor_scalar(stat(13), stat(13), 2.0, 1.0, ALU.mult, ALU.add))
            step(dve.tensor_tensor(stat(0), stat(5), stat(16), ALU.mult))
            step(dve.tensor_tensor(stat(0), stat(0), stat(13), ALU.add))
            step(dve.tensor_scalar(stat(0), stat(0), EPS1, None, ALU.max))
            step(dve.reciprocal(stat(1), stat(0)))
            step(dve.tensor_tensor(stat(13), stat(13), stat(16), ALU.add))
            step(dve.tensor_tensor(stat(13), stat(13), stat(1), ALU.mult))
            step(dve.tensor_tensor(stat(6), stat(6), stat(15), ALU.mult))
            step(dve.tensor_tensor(stat(6), stat(6), stat(1), ALU.mult))
            step(dve.tensor_tensor(xc, xc, over_features(stat(6)), ALU.mult))
            step(dve.tensor_tensor(sq, h_feat, over_features(stat(13)), ALU.mult))
            step(dve.tensor_tensor(xc, xc, sq, ALU.add))
            dve.tensor_tensor(xs[:, :, :], xs[:, :, :], xc, ALU.add).then_inc(S["layer1_done"], 1)
            v.wait_ge(S["layer1_done"], 1)

            layer_norm(4)
            dve.tensor_scalar(h_feat, xc, 0.0, None, ALU.max).then_inc(S["feat_ready"], 1)
            v.wait_ge(S["wa_ready"], 1)
            dve.tensor_copy(w2_sb[:, D:D + 2], ps[0:D, 4, 0:2]).then_inc(S["wa_set"], 1)
            v.wait_ge(S["wh_ready"], 1)
            for b in range(3):
                n = min(PER_BANK, T - PER_BANK * b)
                a = slice(PER_BANK * b, PER_BANK * b + n)
                src = ps[:, 5 + b, 0:n * AUG].rearrange("p (t f) -> p t f", t=n)
                dve.tensor_copy(wh[:, a, 0:D], src[:, :, 0:D])
                dve.tensor_copy(st[:, 15, a], src[:, :, D])
                step(dve.tensor_copy(st[:, 16, a], src[:, :, D + 1]))
            dve.memset(wh[:, :, D:D + 1], 1.0)
            step(dve.tensor_scalar(stat(17), stat(16), ALPHA, None, ALU.mult))
            step(dve.tensor_scalar(stat(19), stat(16), 1.0 - ALPHA, None, ALU.mult))
            step(dve.tensor_scalar(stat(13), stat(17), -1.0, None, ALU.mult))
            dve.tensor_reduce(st[:, 18, 0:1], stat(16), X, ALU.min).then_inc(S["min_ready"], 1)
            v.wait_ge(S["min_t"], 1)
            dve.tensor_reduce(st[0:1, 18, 1:2], ps[0:1, 4, 0:P], X, ALU.min).then_inc(S["min_r"], 1)
            v.wait_ge(S["min_b"], 1)
            step(dve.tensor_copy(st[:, 18, 2:3], ps[:, 4, P:P + 1]))
            step(dve.tensor_scalar(stat(22), stat(16), st[:, 18, 2:3], None, ALU.subtract))
            step(dve.tensor_scalar(best, mask8[:, 0, :], st[:, 22, 0:1], None, ALU.mult))
            for j in range(1, T):
                ins = dve.scalar_tensor_tensor(best, mask8[:, j, :], st[:, 22, j:j + 1], best, ALU.mult, ALU.max)
                if j < T - 1:
                    step(ins)
            ins.then_inc(S["best_ready"], 1)
            v.wait_ge(S["bt_ready"], 1)
            step(dve.tensor_reduce(stat(0), ps[:, 0:NC, :].rearrange("p b (k i) -> p (b k) i", k=TC), X, ALU.max))
            step(dve.tensor_scalar(stat(0), stat(0), st[:, 18, 2:3], None, ALU.add))
            step(dve.tensor_tensor(stat(0), stat(0), stat(15), ALU.add))
            step(dve.scalar_tensor_tensor(stat(0), stat(0), ALPHA, stat(0), ALU.mult, ALU.max))
            step(dve.tensor_tensor(stat(20), stat(15), stat(0), ALU.subtract))
            dve.scalar_tensor_tensor(stat(21), stat(15), ALPHA, stat(0), ALU.mult, ALU.subtract)\
                .then_inc(S["m_ready"], 1)
            v.wait_ge(S["rows_ready"], 2)
            dve.tensor_copy(row_2.rearrange("p (b c) -> p b c", b=NC), ps[:, NC:2 * NC, :]).then_inc(S["row1_set"], 1)
            v.wait_ge(S["row1_set"], 2)
            for j in range(T + 1):
                if j < T:
                    if j >= R:
                        v.wait_ge(S["sum2_done"], j - R + 1)
                    dve.scalar_tensor_tensor(p_ring[j % R], row_1, st[:, 19, j:j + 1], row_2, ALU.add, ALU.max)\
                        .then_inc(S["z_ready"], 1)
                if j >= 1 and j - 1 not in POOL_J:
                    v.wait_ge(S["pe_ready"], j)
                    dve.scalar_tensor_tensor(p_ring[(j - 1) % R], mask8[:, j - 1, :], 2.0, p_ring[(j - 1) % R],
                                             ALU.mult, ALU.min).then_inc(S["pm_ready"], 1)
            sums_turned(2, agg2, D + 1)
            step(dve.reciprocal(stat(0), agg2[:, :, D]))
            step(dve.tensor_tensor(xc, agg2[:, :, 0:D], over_features(stat(0)), ALU.mult))
            dve.tensor_scalar(sq, xc, 0.0, None, ALU.min).then_inc(S["elu_ready"], 1)
            step(dve.scalar_tensor_tensor(xs[:, :, :], xc, 0.0, xs[:, :, :], ALU.max, ALU.add))
            v.wait_ge(S["elu_exp"], 1)
            step(dve.scalar_tensor_tensor(xs[:, :, :], sq, -1.0, xs[:, :, :], ALU.add, ALU.add))

            layer_norm(5)
            dve.tensor_scalar(h_feat, xc, 0.0, None, ALU.max).then_inc(S["feat_ready"], 1)
            v.wait_ge(S["h3_ready"], 1)
            src = ps[:, 4:8, :].rearrange("p b (k f) -> p (b k) f", k=TC)
            step(dve.tensor_copy(parts3[:, :, 0:D], src[:, :, 0:D]))
            step(dve.tensor_tensor(r3, src[:, :, 0:D], parts3[:, :, 0:D], ALU.subtract))
            step(dve.tensor_copy(parts3[:, :, D:2 * D], r3))
            dve.memset(parts3[:, :, 3 * D:PW], 1.0)
            dve.tensor_tensor(parts3[:, :, 2 * D:3 * D], r3, parts3[:, :, D:2 * D], ALU.subtract)\
                .then_inc(S["parts_ready"], 1)
            step(dve.tensor_tensor(self3, src[:, :, D:2 * D], xs[:, :, :], ALU.add))
            step(dve.tensor_tensor(self3, self3, bias_sb[:, :].unsqueeze(1).to_broadcast([P, T, D]), ALU.add))
            for g in range(T // 2):
                a = slice(2 * g, 2 * g + 2)
                v.wait_ge(S["sum3_ready"], g + 1)
                acc = ps[:, g % 4, 0:2 * PW].rearrange("p (t f) -> p t f", t=2)
                step(dve.reciprocal(st[:, 23, a], acc[:, :, 3 * D]))
                dve.tensor_reduce(r3[:, a, :], acc[:, :, 0:3 * D].rearrange("p t (s f) -> p t f s", s=3), X, ALU.add)\
                    .then_inc(S["sum3_read"], 1)
                v.wait_ge(S["sum3_read"], g + 1)
                step(dve.tensor_tensor(r3[:, a, :], r3[:, a, :], st[:, 23, a].unsqueeze(2).to_broadcast([P, 2, D]),
                                       ALU.mult))
                ins = dve.tensor_tensor(xs[:, a, :], r3[:, a, :], self3[:, a, :], ALU.add)
                if g % 4 == 3:
                    ins.then_inc(S["y_ready"], 1)


def kernel(x, adj, L0_gnn_w_k, L0_gnn_w_q, L2_gnn_W, L2_gnn_a, L3_gnn_weight, L3_gnn_bias):
    import numpy as np
    import concourse.bacc as bacc
    from concourse.bass_utils import run_bass_kernel_spmd as run

    sel = np.zeros((P, 4), np.float32)
    for r in range(KP):
        a, b = r // EMB // 3, r // EMB % 3
        sel[r] = (-(a > 0), -(a > 1), -(b > 0), -(b > 1))
    f = np.asarray
    arrays = {
        "x": np.ascontiguousarray(f(x)),
        "adj_t": np.ascontiguousarray(f(adj).T),
        "w_k": np.ascontiguousarray(f(L0_gnn_w_k)),
        "w_q": np.ascontiguousarray(f(L0_gnn_w_q)),
        "w2": np.ascontiguousarray(f(L2_gnn_W)),
        "w2_t": np.ascontiguousarray(f(L2_gnn_W).T),
        "a2": np.ascontiguousarray(f(L2_gnn_a).reshape(2, D).T),
        "w3": np.ascontiguousarray(f(L3_gnn_weight)),
        "bias3": np.ascontiguousarray(f(L3_gnn_bias)),
        "sel": sel,
        "ident": np.eye(P, dtype=np.float32),
    }
    nc = bacc.Bacc("TRN2", target_bir_lowering=False, num_devices=1)
    args = [nc.dram_tensor("in_" + n, a.shape, mybir.dt.from_np(a.dtype), kind="ExternalInput").ap()
            for n, a in arrays.items()]
    out = nc.dram_tensor("out", (N, D), F32, kind="ExternalOutput").ap()
    build(nc, *args, out)
    r = run(nc, [{"in_" + n: a for n, a in arrays.items()}], core_ids=[0])
    return r.results[0]["out"]
```

```python
from contextlib import ExitStack

import concourse.bass as bass
from concourse import mybir

P = 128
N = 2048
D = 64
T = N // P
EMB = 8
CH = 512
NC = N // CH
TC = CH // P
KP = 9 * EMB
MROW = 96
KM = MROW + 3
AUG = D + 2
LN_EPS = 1e-5
EPS0 = 1e-12
EPS1 = 1e-7
UMAX = 1.0 - 1e-5
DMIN = 1e-9
ALPHA = 0.2
R = 6
W_LAG, LO_LAG, SUM_LAG = 4, 5, 6

F32 = mybir.dt.float32
BF16 = mybir.dt.bfloat16
F8 = mybir.dt.float8e4
I32 = mybir.dt.int32
ALU = mybir.AluOpType
ACT = mybir.ActivationFunctionType
X = mybir.AxisListType.X

TRI = [(j, i) for j in range(T) for i in range(j, T)]
CHUNKS = [TRI[c:c + TC] for c in range(0, len(TRI), TC)]
NCH = len(CHUNKS)
LAST_BANK = 1 + max(c for c, chunk in enumerate(CHUNKS) if any(j < T - TC for j, i in chunk))
CAST = {"g": (0, 2, 7, 9, 11), "v": (3, 4, 5, 6), "a": (1, 8, 10, 12, 13, 14, 15)}
MASK_V = ((1, 4, 7), (1, 4, 7), (1, 3, 5, 6, 7), (1, 3, 5, 6, 7))
MASKS = {"v": [(c, g) for c in range(NC) for g in range(8) if g in MASK_V[c]],
         "g": [(c, g) for c in range(NC) for g in range(8) if g not in MASK_V[c]]}
POOL_J = (1, 2, 4, 5, 7, 8, 10, 11, 13, 14)
R2 = 6
PM_LAG = 3
BEST_G = 4
ABSENT = 2.0 ** 60
SUB_V = 4
LATE = 3


def on_vector(b):
    return b % SUB_V == SUB_V - 1 or b >= NCH - LATE + 1


def runs(chunk, diagonal):
    out = []
    for s, (j, i) in enumerate(chunk):
        if i == j and not diagonal:
            continue
        if out and out[-1][2] == j and out[-1][0] + out[-1][1] == s:
            out[-1][1] += 1
        else:
            out.append([s, 1, j, i])
    return out


def build(nc, x, adj_t, w_k, w_q, w2, w2_t, a2, w3, bias3, sel, ident, out):
    ctx = ExitStack()
    with ctx:
        def sb(name, shape, dt=F32):
            return ctx.enter_context(nc.sbuf_tensor(name, shape, dt))

        def sem(name):
            return ctx.enter_context(nc.semaphore(name))

        ps = ctx.enter_context(nc.psum_tensor("ps", [P, 8, CH], F32))

        big = sb("big", [P, T * N])
        mask8 = sb("mask8", [P, T, N], F8)
        ht = sb("ht", [P, N])
        scratch = sb("scratch", [P, N])
        k_part = sb("k_part", [P, N], BF16)
        q_part = sb("q_part", [P, N], BF16)
        rounded = [sb(f"rounded_{n}", [P, N], BF16) for n in range(2)]
        xs = sb("xs", [P, T, D])
        feat = sb("feat", [P, T, AUG])
        idf = sb("idf", [P, P])
        idb = sb("idb", [P, P], BF16)
        wk_rep = sb("wk_rep", [P, 9, EMB])
        wq_rep = sb("wq_rep", [P, 9, EMB])
        wkq = sb("wkq", [D, 2, EMB])
        sel_sb = sb("sel_sb", [P, 4])
        w2_sb = sb("w2_sb", [P, AUG])
        w2t_sb = sb("w2t_sb", [D, D])
        a2_sb = sb("a2_sb", [D, 2])
        w3_sb = sb("w3_sb", [P, 2, D])
        bias_sb = sb("bias_sb", [P, D])
        st = sb("st", [P, 24, T])
        rowmax = sb("rowmax", [P, T, 2])
        m_parts = sb("m_parts", [P, T, 3], BF16)
        ones = sb("ones", [P, P // NC])
        one_col = sb("one_col", [P, 1])

        attn = big[:, :].rearrange("p (j i) -> p j i", j=T)
        adj_stage = big[:, :].bitcast(I32).rearrange("p (j i) -> p j i", j=T)
        ut_buf = rounded[0][:, :].bitcast(F32).rearrange("p (b c) -> p b c", b=2)
        u_buf = [ht[:, b * T * D:(b + 1) * T * D].rearrange("p (t f) -> p t f", t=T) for b in range(2)]
        xc = scratch[:, 0:T * D].rearrange("p (t f) -> p t f", t=T)
        sq = scratch[:, T * D:2 * T * D].rearrange("p (t f) -> p t f", t=T)
        h_feat = feat[:, :, 0:D]

        cut = [0]

        def carve(n):
            cut[0] += n
            return big[:, cut[0] - n:cut[0]]
        feat_a = [m[:, :].bitcast(F32)[:, 0:T // 2 * AUG].rearrange("p (t f) -> p t f", t=T // 2)
                  for m in (q_part, k_part)]
        xt, xa, b_row = carve(N), carve(N), carve(N)
        ring = {n: [carve(CH) for _ in range(R)] for n in
                ("den", "dist", "prod", "inv_s", "atn", "w", "w_up", "w_lo")}
        assert cut[0] <= T * N
        cut[0] = 0
        row_1, row_2, best = carve(N), carve(N), carve(N)
        p_ring = [carve(N) for _ in range(R2)]
        wh = carve(T * D).rearrange("p (t f) -> p t f", t=T)
        bias2 = [carve(N // 2).bitcast(BF16) for _ in POOL_J]
        assert cut[0] <= T * N
        cut[0] = 0
        self3 = carve(T * D).rearrange("p (t f) -> p t f", t=T)
        r3 = carve(T * D).rearrange("p (t f) -> p t f", t=T)
        PW = 3 * D + 1
        parts3 = carve(T * (PW + 1) // 2).bitcast(BF16)[:, 0:T * PW].rearrange("p (t f) -> p t f", t=T)
        assert cut[0] <= 6 * N

        def stat(n):
            return st[:, n, :]

        def over_features(ap, n=T):
            return ap.unsqueeze(2).to_broadcast([P, n, D])

        def by_tile(bank, width=P):
            return ps[:, bank:bank + NC, :].rearrange("p b (k f) -> p (b k) f", k=TC)[:, :, 0:width]

        S = {}
        for names in (
                "x_in w_in const_set cast_g cast_a cast_v step var_ready std_ready feat_ready "
                "tr_ready ht_ready",
                "rep_ready rnd_ready part_ready gmax_ready gmax_read mcol_ready mrow_ready mrow_set "
                "score_ready exp_ready masked_v masked_g u_summed u_copied u_turned u_ready",
                "pad_set brow_ready brow_set operand_turned xt_ready xa_ready xa_late gram_ready "
                "gram_read den_ready den_held product_ready lnp_ready invs_ready u_norm_ready "
                "ln1_ready ln_ready atn_ready w_ready wt_ready wlo_ready wup_ready wup_late sum1_done "
                "aggt_ready aggt_back square_ready norm_ready angle_ready tanh_ready coef_x along_x",
                "wa_ready wa_set wh_ready min_ready min_t min_r min_b spread_ready above_ready best_a "
                "best_g best_ready best_turned m_ready rows_ready row1_set row2_set bias2_ready "
                "z_ready z_masked exp2_ready masked2_ready sum2_done elu_ready elu_exp",
                "h3_ready parts_ready sum3_ready sum3_read y_ready out_done"):
            S.update({n: sem(n) for n in names.split()})
        adj_in = [sem(f"adj_in_{j}") for j in range(T)]

        block = ctx.enter_context(nc.Block())

        agg_t = scratch[:, :]

        AHEAD = 2

        @block.sync
        def _(sp):
            sp.dma_start(xs[:, :, :], x.rearrange("(t p) f -> p t f", p=P)).then_inc(S["x_in"], 16)
            for dst, src in ((idf[:, :], ident), (sel_sb[:, :], sel), (wkq[:, 0, :], w_k), (wkq[:, 1, :], w_q),
                             (w2_sb[0:D, 0:D], w2), (w2t_sb[:, :], w2_t), (a2_sb[:, :], a2),
                             (w3_sb[0:D, :, :], w3.rearrange("(s k) f -> k s f", s=2)),
                             (bias_sb[:, :], bias3.partition_broadcast(P))):
                sp.dma_start(dst, src).then_inc(S["w_in"], 16)
            for j in range(T):
                sp.dma_start(adj_stage[:, j, :], adj_t[j * P:(j + 1) * P, :]).then_inc(adj_in[j], 16)
            for h in range(2):
                sp.wait_ge(S["y_ready"], h + 1)
                sp.dma_start(out.rearrange("(t p) f -> p t f", p=P)[:, h * 8:h * 8 + 8, :],
                             xs[:, h * 8:h * 8 + 8, :]).then_inc(S["out_done"], 16)
            sp.wait_ge(S["out_done"], 32)

        W_IN = 16 * 9

        @block.gpsimd
        def _(pool):
            nc.gpsimd.memset(k_part[:, :], 0.0).then_inc(S["const_set"], 1)
            nc.gpsimd.memset(q_part[:, :], 0.0).then_inc(S["const_set"], 1)
            nc.gpsimd.memset(feat[:, :, D:D + 1], 1.0).then_inc(S["const_set"], 1)
            nc.gpsimd.memset(one_col[:, :], 1.0).then_inc(S["const_set"], 1)
            nc.gpsimd.memset(ones[:, :], 1.0).then_inc(S["const_set"], 1)
            pool.wait_ge(S["const_set"], 5)
            nc.gpsimd.memset(ht[D:P, :], 0.0).then_inc(S["const_set"], 1)
            for w in (wk_rep, wq_rep, w3_sb):
                nc.gpsimd.memset(w[D:P, :, :], 0.0).then_inc(S["const_set"], 1)
            nc.gpsimd.memset(w2_sb[D:P, :], 0.0).then_inc(S["const_set"], 1)
            pool.wait_ge(S["const_set"], 10)
            nc.gpsimd.memset(q_part[MROW:KM, :], -1.0).then_inc(S["const_set"], 1)
            pool.wait_ge(S["const_set"], 11)
            for j in CAST["g"]:
                pool.wait_ge(adj_in[j], 16)
                nc.gpsimd.tensor_copy(mask8[:, j, :], adj_stage[:, j, :], saturate=False)\
                    .then_inc(S["cast_g"], 1)
            for c, g in MASKS["g"]:
                pool.wait_ge(S["exp_ready"], T * c + 2 * g + 2)
                e = attn[:, 2 * g:2 * g + 2, c * CH:(c + 1) * CH]
                nc.gpsimd.tensor_tensor(e, e, mask8[:, 2 * g:2 * g + 2, c * CH:(c + 1) * CH],
                                        ALU.mult).then_inc(S["masked_g"], 1)
            pool.wait_ge(S["u_summed"], 8)
            for h in range(2):
                for m in (xt, xa):
                    nc.gpsimd.memset(m[D:P, h * N // 2:(h + 1) * N // 2], 0.0).then_inc(S["pad_set"], 1)
            pool.wait_ge(S["feat_ready"], 3)
            nc.gpsimd.memset(ht[D:P, :], 0.0).then_inc(S["pad_set"], 1)
            pool.wait_ge(S["pad_set"], 5)
            for c in range(NCH + W_LAG):
                if c < NCH:
                    pool.wait_ge(S["invs_ready"], c + 1)
                    nc.gpsimd.tensor_tensor(ring["dist"][c % R], ring["dist"][c % R], ring["inv_s"][c % R],
                                            ALU.mult).then_inc(S["u_norm_ready"], 1)
                if 1 <= c <= NCH and not on_vector(c - 1):
                    b = c - 1
                    pool.wait_ge(S["ln_ready"], b + 1)
                    nc.gpsimd.tensor_tensor(ring["atn"][b % R], ring["atn"][b % R], ring["dist"][b % R],
                                            ALU.subtract).then_inc(S["atn_ready"], 1)
                if W_LAG <= c < NCH - LATE + W_LAG:
                    b = c - W_LAG
                    pool.wait_ge(S["w_ready"], b + 1)
                    if b >= R:
                        pool.wait_ge(S["sum1_done"], b - R + 1)
                    for s, n, j, i in runs(CHUNKS[b], True):
                        nc.gpsimd.tensor_tensor(ring["w_up"][b % R][:, s * P:(s + n) * P],
                                                ring["w"][b % R][:, s * P:(s + n) * P],
                                                mask8[:, j, i * P:(i + n) * P], ALU.mult).then_inc(S["wup_ready"], 1)
            pool.wait_ge(S["coef_x"], 1)
            nc.gpsimd.tensor_tensor(sq, h_feat, over_features(stat(13)), ALU.mult).then_inc(S["along_x"], 1)
            tiles = p_ring[0:BEST_G]
            for n, (ready, dst, src, op) in enumerate((
                    (2, 1, 0, ALU.subtract), (4, 3, 2, ALU.subtract), (5, 0, 1, ALU.add), (6, 2, 3, ALU.add))):
                pool.wait_ge(S["best_a"], ready)
                pool.wait_ge(S["best_g"], n)
                nc.gpsimd.tensor_tensor(tiles[dst], tiles[dst], tiles[src], op).then_inc(S["best_g"], 1)
            for n, j in enumerate(POOL_J):
                pool.wait_ge(S["bias2_ready"], n + 1)
                pool.wait_ge(S["z_ready"], j + 1)
                nc.gpsimd.tensor_tensor(p_ring[j % R2], p_ring[j % R2], bias2[n], ALU.add)\
                    .then_inc(S["z_masked"], 1)

        wup_count = [0]
        for ch in CHUNKS:
            wup_count.append(wup_count[-1] + len(runs(ch, True)))

        @block.scalar
        def _(act):
            def root(ready, value, dst, src, done):
                act.wait_ge(S[ready], value)
                nc.scalar.activation(dst, src, ACT.Sqrt).then_inc(S[done], 1)

            def transposed(tr0):
                for g in range(NC):
                    act.wait_ge(S["tr_ready"], tr0 + g + 1)
                    nc.scalar.copy(ht[0:D, g * CH:(g + 1) * CH], ps[0:D, g, :]).then_inc(S["ht_ready"], 1)

            def cast(j):
                act.wait_ge(adj_in[j], 16)
                nc.scalar.activation(mask8[:, j, :], adj_stage[:, j, :], ACT.Copy, saturate=False)\
                    .then_inc(S["cast_a"], 1)

            cast(1)
            root("var_ready", 1, stat(3), stat(2), "std_ready")
            transposed(0)
            for m in range(2):
                for n in range(2):
                    act.wait_ge(*((S["rep_ready"], n + 1) if m == 0 else (S["part_ready"], n + 1)))
                    nc.scalar.copy(rounded[n][0:KP, :].rearrange("p (b c) -> p b c", b=NC),
                                   ps[0:KP, 4 * n:4 * n + 4, :]).then_inc(S["rnd_ready"], 1)
            nc.scalar.preload_act_table_set("exp_and_others")
            early = [j for j in CAST["a"] if j < T - 1]
            for j in early[1:]:
                cast(j)
            def weights_0(c, j):
                act.wait_ge(S["score_ready"], T * c + j + 1)
                nc.scalar.activation(attn[:, j, bass.ds(c * CH, CH)], ps[:, 4 + j % 2, :],
                                     ACT.Exp, scale=EMB ** -0.5).then_inc(S["exp_ready"], 1)

            act.wait_ge(S["mrow_ready"], 1)
            nc.scalar.copy(k_part[MROW:KM, 0:CH], ps[MROW:KM, 7, :]).then_inc(S["mrow_set"], 1)
            for j in range(T):
                if j in CAST["g"]:
                    act.wait_ge(S["cast_g"], CAST["g"].index(j) + 1)
                elif j in CAST["v"]:
                    act.wait_ge(S["cast_v"], CAST["v"].index(j) + 1)
                else:
                    act.wait_ge(S["cast_a"], CAST["a"].index(j) + 1)
                weights_0(0, j)
                if j == T - 3:
                    cast(T - 1)
            with act.Fori(1, NC) as c:
                act.wait_ge(S["mrow_ready"], c + 1)
                nc.scalar.copy(k_part[MROW:KM, bass.ds(c * CH, CH)], ps[MROW:KM, 7, :]).then_inc(S["mrow_set"], 1)
                for j in range(T):
                    weights_0(c, j)
            for n in range(8):
                act.wait_ge(S["u_summed"], n + 1)
                if n >= 2:
                    act.wait_ge(S["u_turned"], n - 1)
                nc.scalar.copy(ut_buf[:, n % 2, :], ps[:, 6 + n % 2, :]).then_inc(S["u_copied"], 1)
                if n == 6:
                    root("var_ready", 2, st[:, 3, 0:T // 2], st[:, 2, 0:T // 2], "std_ready")

            def to_operand(g, n):
                act.wait_ge(S["operand_turned"], 2 * g + n + 1)
                act.wait_ge(S["pad_set"], 2 * (g // 2) + n + 1)
                nc.scalar.copy((xt, xa)[n][0:AUG, g * CH:(g + 1) * CH], ps[0:AUG, 2 * (g % 2) + n, :])\
                    .then_inc(S["xa_ready" if n else "xt_ready"], 1)

            def b_to_row(h):
                act.wait_ge(S["brow_ready"], h + 1)
                nc.scalar.copy(b_row.rearrange("p (b c) -> p b c", b=NC)[:, 2 * h:2 * h + 2, :],
                               ps[:, 4 + 2 * h:6 + 2 * h, :]).then_inc(S["brow_set"], 1)

            for g in range(2):
                for n in range(2):
                    to_operand(g, n)
                if g == 0:
                    b_to_row(0)
            root("var_ready", 3, st[:, 3, T // 2:T], st[:, 2, T // 2:T], "std_ready")
            nc.scalar.preload_act_table_set("natural_log_exp_and_others")
            to_operand(2, 0)
            b_to_row(1)
            to_operand(3, 0)
            def inverse_root(c, slot):
                act.wait_ge(S["product_ready"], c + 1)
                nc.scalar.activation(ring["prod"][slot], ring["prod"][slot], ACT.Ln,
                                     scale=1.0 / UMAX ** 2).then_inc(S["lnp_ready"], 1)
                act.wait_ge(S["lnp_ready"], c + 1)
                nc.scalar.activation(ring["inv_s"][slot], ring["prod"][slot], ACT.Exp,
                                     scale=-0.5).then_inc(S["invs_ready"], 1)

            def logarithms(b, slot):
                act.wait_ge(S["u_norm_ready"], b + 1)
                nc.scalar.activation(ring["atn"][slot], ring["dist"][slot], ACT.Ln, bias=one_col[:, :])\
                    .then_inc(S["ln1_ready"], 1)
                act.wait_ge(S["ln1_ready"], b + 1)
                nc.scalar.activation(ring["dist"][slot], ring["dist"][slot], ACT.Ln, bias=one_col[:, :],
                                     scale=-1.0).then_inc(S["ln_ready"], 1)

            for c in range(R):
                inverse_root(c, c)
                if c >= 1:
                    logarithms(c - 1, c - 1)
            with act.Fori(R, NCH - NCH % R, R) as c0:
                for k in range(R):
                    act.wait_ge(S["w_ready"], c0 + (k - R + 1))
                    inverse_root(c0 + k, k)
                    logarithms(c0 + (k - 1), (k - 1) % R)
            for c in range(NCH - NCH % R, NCH + 1):
                if c < NCH:
                    act.wait_ge(S["w_ready"], c - R + 1)
                    inverse_root(c, c % R)
                logarithms(c - 1, (c - 1) % R)
            for chunks, a, b in ((LAST_BANK, 0, NC - 1), (NCH, NC - 1, NC)):
                act.wait_ge(S["sum1_done"], chunks)
                nc.scalar.copy(agg_t[0:AUG, a * CH:b * CH].rearrange("p (b c) -> p b c", c=CH),
                               ps[0:AUG, 4 + a:4 + b, :]).then_inc(S["aggt_ready"], 1)
            root("square_ready", 1, stat(8), stat(7), "norm_ready")
            act.wait_ge(S["angle_ready"], 1)
            nc.scalar.activation(stat(11), stat(10), ACT.Tanh).then_inc(S["tanh_ready"], 1)
            root("var_ready", 4, stat(3), stat(2), "std_ready")
            transposed(4)
            def absent(n):
                nc.scalar.activation(bias2[n], mask8[:, POOL_J[n], :], ACT.Copy, scale=ABSENT, bias=-ABSENT)\
                    .then_inc(S["bias2_ready"], 1)

            def positive(k, after):
                act.wait_ge(S["best_g"], after)
                nc.scalar.activation(p_ring[k], p_ring[k], ACT.Relu).then_inc(S["best_a"], 1)

            act.wait_ge(S["above_ready"], 1)
            for k in range(BEST_G):
                j = T - BEST_G + k
                nc.scalar.activation(p_ring[k], mask8[:, j, :], ACT.Copy, scale=st[:, 22, j:j + 1])\
                    .then_inc(S["best_a"], 1)
            positive(1, 1)
            act.wait_ge(S["rows_ready"], NC)
            nc.scalar.copy(row_1.rearrange("p (b c) -> p b c", b=NC), ps[:, NC:2 * NC, :]).then_inc(S["row1_set"], 1)
            positive(3, 2)
            for n in range(len(POOL_J)):
                absent(n)
            for c in range(NC):
                act.wait_ge(S["rows_ready"], NC + c + 1)
                nc.scalar.copy(row_2[:, c * CH:(c + 1) * CH], ps[:, NC + c, :]).then_inc(S["row2_set"], 1)
            for j in range(T):
                if j in POOL_J:
                    act.wait_ge(S["z_masked"], POOL_J.index(j) + 1)
                else:
                    act.wait_ge(S["z_ready"], j + 1)
                nc.scalar.activation(p_ring[j % R2], p_ring[j % R2], ACT.Exp,
                                     bias=st[:, 17, j:j + 1]).then_inc(S["exp2_ready"], 1)
            act.wait_ge(S["sum2_done"], T)
            for n in (2, 0, 1):
                nc.scalar.copy(agg_t[:, n * CH:(n + 1) * CH], ps[:, 4 + n, :]).then_inc(S["aggt_ready"], 1)
            act.wait_ge(S["elu_ready"], 1)
            nc.scalar.activation(sq, sq, ACT.Exp).then_inc(S["elu_exp"], 1)
            root("var_ready", 5, stat(3), stat(2), "std_ready")
            transposed(8)

        @block.tensor
        def _(pe):
            def transposes(src, g, bank, width):
                for k in range(TC):
                    last = nc.tensor.transpose(ps[0:width, bank, k * P:(k + 1) * P], src[:, TC * g + k, :], idf[:, :])
                return last

            pe.wait_ge(S["w_in"], W_IN)
            pe.wait_ge(S["feat_ready"], 1)
            for g in range(NC):
                transposes(h_feat, g, g, D).then_inc(S["tr_ready"], 1)
            pe.wait_ge(S["wa_set"], 1)
            for n, w in enumerate((wk_rep, wq_rep)):
                for g in range(NC):
                    pe.wait_ge(S["ht_ready"], g + 1 if n else NC)
                    last = nc.tensor.matmul(ps[0:KP, 4 * n + g, :], w[:, :, :], ht[:, g * CH:(g + 1) * CH],
                                            start=True, stop=True)
                last.then_inc(S["rep_ready"], 1)
            pe.wait_ge(S["part_ready"], 4)

            def group_max(n):
                if n >= 2:
                    pe.wait_ge(S["gmax_read"], n - 1)
                for h in range(2):
                    t, q = n // 2, 2 * (n % 2) + h
                    last = nc.tensor.matmul(ps[:, 2 * (n % 2) + h, :], k_part[:, t * P:(t + 1) * P],
                                            q_part[:, q * CH:(q + 1) * CH], start=True, stop=True)
                last.then_inc(S["gmax_ready"], 1)

            def group_score(n):
                for h in range(2):
                    c, j = n // 8, 2 * (n % 8) + h
                    if 2 * n + h >= 2:
                        pe.wait_ge(S["exp_ready"], 2 * n + h - 1)
                    nc.tensor.matmul(ps[:, 4 + h, :], q_part[:, j * P:(j + 1) * P],
                                     k_part[:, c * CH:(c + 1) * CH], start=True, stop=True)\
                        .then_inc(S["score_ready"], 1)

            def propagate(n, j):
                k, pair = 1 + n // 2, n % 2
                if k == 1 and j % 2 == 0:
                    for c in (2 * pair, 2 * pair + 1):
                        who = "v" if (c, j // 2) in MASKS["v"] else "g"
                        pe.wait_ge(S["masked_" + who], MASKS[who].index((c, j // 2)) + 1)
                    if pair:
                        pe.wait_ge(S["mrow_set"], NC)
                if k > 1 and pair == 0 and j % 8 == 0:
                    pe.wait_ge(S["u_ready"], n - 2 + j // 8 + 1)
                src = feat[:, j, 1:D + 1] if k == 1 else u_buf[k % 2][:, j, :]
                for h in range(2):
                    c = 2 * pair + h
                    last = nc.tensor.matmul(ps[h * D:(h + 1) * D, 6 + n % 2, :], src,
                                            attn[:, j, c * CH:(c + 1) * CH], start=(j == 0), stop=(j == T - 1))
                if j == T - 1:
                    last.then_inc(S["u_summed"], 1)

            def turn_pair(n):
                pe.wait_ge(S["u_copied"], n + 1)
                if n >= 2:
                    pe.wait_ge(S["u_ready"], n - 1)
                else:
                    pe.wait_ge(S["gmax_read"], 8 * NC)
                for k in range(TC):
                    last = nc.tensor.transpose(ps[:, 2 + n % 2, k * P:(k + 1) * P],
                                               ut_buf[:, n % 2, k * P:(k + 1) * P], idf[:, :])
                last.then_inc(S["u_turned"], 1)

            for m in range(8 * NC + 8 + AHEAD):
                if m < 8 * NC:
                    group_max(m)
                n = m - 8 - AHEAD
                if n < 0:
                    continue
                if n % 8 == 0:
                    c = n // 8
                    pe.wait_ge(S["mcol_ready"], c + 1)
                    if c:
                        pe.wait_ge(S["mrow_set"], c)
                    for k in range(TC):
                        last = nc.tensor.matmul(ps[MROW:KM, 7, k * P:(k + 1) * P],
                                                m_parts[:, TC * c + k, :], idb[:, :], start=True, stop=True)
                    last.then_inc(S["mrow_ready"], 1)
                    pe.wait_ge(S["mrow_set"], c + 1)
                group_score(n)
                if n >= 16:
                    propagate(0, n - 16)
            for n in range(1, 8):
                for j in range(T):
                    if j == 4:
                        turn_pair(n - 1)
                    propagate(n, j)

            def b_row_of(tiles):
                for t in tiles:
                    last = nc.tensor.matmul(ps[:, 4 + t // TC, (t % TC) * P:(t % TC + 1) * P],
                                            st[:, 6, t:t + 1].to_broadcast([P, P]), idf[:, :], start=True, stop=True)
                if tiles[-1] % 8 == 7:
                    last.then_inc(S["brow_ready"], 1)

            def operands(g):
                for n, src in enumerate((feat, feat_a[g // 2])):
                    if g >= 2:
                        pe.wait_ge(S["xa_ready"] if n else S["xt_ready"], g - 1)
                    transposes(src, g % 2 if n else g, 2 * (g % 2) + n, AUG).then_inc(S["operand_turned"], 1)

            pe.wait_ge(S["feat_ready"], 2)
            b_row_of(range(0, 4))
            turn_pair(7)
            operands(0)
            b_row_of(range(4, 8))
            pe.wait_ge(S["u_ready"], 8)
            operands(1)
            pe.wait_ge(S["feat_ready"], 3)
            operands(2)
            b_row_of(range(8, 16))
            operands(3)

            def gram(c):
                if c == 0:
                    pe.wait_ge(S["xt_ready"], 3)
                    pe.wait_ge(S["xa_late"], 1)
                if c == 1:
                    pe.wait_ge(S["xt_ready"], NC)
                    pe.wait_ge(S["xa_late"], 2)
                if c >= 2:
                    pe.wait_ge(S["gram_read"], c - 1)
                for s, k, j, i in runs(CHUNKS[c], True):
                    last = nc.tensor.matmul(ps[:, c % 2, s * P:(s + k) * P], xa[:, j * P:(j + 1) * P],
                                            xt[:, i * P:(i + k) * P], start=True, stop=True)
                last.then_inc(S["gram_ready"], 1)

            opened = set()

            def add_to(i, k, src, w):
                bank = 4 + i // TC
                first = bank not in opened
                opened.add(bank)
                return nc.tensor.matmul(ps[0:AUG, bank, (i % TC) * P:(i % TC + k) * P], src, w,
                                        start=first, stop=True, skip_group_check=True)

            gram(0)
            pe.wait_ge(S["brow_set"], 2)
            for c in range(NCH + SUM_LAG):
                if c + 1 < NCH:
                    gram(c + 1)
                if c >= SUM_LAG:
                    b = c - SUM_LAG
                    if b < NCH - LATE:
                        pe.wait_ge(S["wup_ready"], wup_count[b + 1])
                    else:
                        pe.wait_ge(S["wup_late"], b - NCH + LATE + 1)
                    for s, k, j, i in runs(CHUNKS[b], True):
                        while k:
                            m = min(k, TC - i % TC)
                            last = add_to(i, m, feat[:, j, :], ring["w_up"][b % R][:, s * P:(s + m) * P])
                            s, k, i = s + m, k - m, i + m
                    pe.wait_ge(S["wlo_ready"], b + 1)
                    for s, (j, i) in enumerate(CHUNKS[b]):
                        if i != j:
                            last = add_to(j, 1, feat[:, i, :], ring["w_lo"][b % R][:, s * P:(s + 1) * P])
                    last.then_inc(S["sum1_done"], 1)
                if W_LAG <= c < NCH + W_LAG:
                    b = c - W_LAG
                    pe.wait_ge(S["w_ready"], b + 1)
                    if b >= 2:
                        pe.wait_ge(S["wlo_ready"], b - 1)
                    last = None
                    for s, (j, i) in enumerate(CHUNKS[b]):
                        if i != j:
                            last = nc.tensor.transpose(ps[:, 2 + b % 2, s * P:(s + 1) * P],
                                                       ring["w"][b % R][:, s * P:(s + 1) * P], idf[:, :])
                    if last is None:
                        pe.sem_inc(S["wt_ready"], 1)
                    else:
                        last.then_inc(S["wt_ready"], 1)

            for t in range(T):
                if t % 12 == 0:
                    pe.wait_ge(S["aggt_ready"], 1 + t // 12)
                last = nc.tensor.transpose(ps[:, t // TC, (t % TC) * P:(t % TC) * P + AUG],
                                           agg_t[0:AUG, t * P:(t + 1) * P], idf[0:AUG, 0:AUG])
            last.then_inc(S["aggt_back"], 1)

            def through(first_feat, first_ht, product):
                for g in range(NC):
                    pe.wait_ge(S["feat_ready"], first_feat + g)
                    transposes(h_feat, g, g, D).then_inc(S["tr_ready"], 1)
                for g in range(NC):
                    pe.wait_ge(S["ht_ready"], first_ht + g + 1)
                    product(g)

            nc.tensor.matmul(ps[0:D, 4, 0:2], w2t_sb[:, :], a2_sb[:, :], start=True, stop=True)\
                .then_inc(S["wa_ready"], 1)
            def wh_product(g):
                if g == 0:
                    pe.wait_ge(S["wa_set"], 2)
                    pe.wait_ge(S["pad_set"], 5)
                for k in range(TC):
                    t = TC * g + k
                    last = nc.tensor.matmul(ps[:, 4 + g, k * P:k * P + AUG], ht[:, t * P:(t + 1) * P], w2_sb[:, :],
                                            start=True, stop=True)
                if g == NC - 1:
                    last.then_inc(S["wh_ready"], 1)

            through(4, NC, wh_product)
            pe.wait_ge(S["min_ready"], 1)
            nc.tensor.transpose(ps[0:1, 0, 0:P], stat(18)[:, 0:1], idf[:, :]).then_inc(S["min_t"], 1)
            pe.wait_ge(S["min_r"], 1)
            nc.tensor.matmul(ps[:, 0, P:P + 1], one_col[0:1, 0:1].to_broadcast([1, P]), st[0:1, 18, 1:2],
                             start=True, stop=True)\
                .then_inc(S["min_b"], 1)
            def row_of(n):
                for t in range(T):
                    last = nc.tensor.matmul(ps[:, 4 + t // TC, (t % TC) * P:(t % TC + 1) * P],
                                            st[:, n, t:t + 1].to_broadcast([P, P]), idf[:, :],
                                            start=True, stop=True)
                    if t % TC == TC - 1:
                        last.then_inc(S["rows_ready"], 1)

            pe.wait_ge(S["spread_ready"], 1)
            row_of(20)
            for g in range(NC):
                pe.wait_ge(S["best_ready"], g + 1)
                for t in range(TC * g, TC * g + TC):
                    last = nc.tensor.transpose(ps[:, g, (t % TC) * P:(t % TC + 1) * P],
                                               best[:, t * P:(t + 1) * P], idf[:, :])
                last.then_inc(S["best_turned"], 1)
            pe.wait_ge(S["m_ready"], 1)
            pe.wait_ge(S["row1_set"], 1)
            row_of(21)
            pe.wait_ge(S["row2_set"], NC)
            for j in range(T):
                if j in POOL_J:
                    pe.wait_ge(S["exp2_ready"], j + 1)
                else:
                    pe.wait_ge(S["masked2_ready"], j + 1 - sum(k < j for k in POOL_J))
                for c in range(NC):
                    nc.tensor.matmul(ps[(c % 2) * D:(c % 2 + 1) * D, 4 + c // 2, :], wh[:, j, :],
                                     p_ring[j % R2][:, c * CH:(c + 1) * CH], start=(j == 0), stop=(j == T - 1))
                for c in range(NC):
                    last = nc.tensor.matmul(ps[c * 32:(c + 1) * 32, 6, :], ones[:, :],
                                            p_ring[j % R2][:, c * CH:(c + 1) * CH], start=(j == 0), stop=(j == T - 1))
                last.then_inc(S["sum2_done"], 1)
            for n in (2, 0, 1):
                pe.wait_ge(S["aggt_ready"], (4, 5, 3)[n])
                for k in range(TC):
                    last = nc.tensor.transpose(ps[:, n, k * P:(k + 1) * P],
                                               agg_t[:, n * CH + k * P:n * CH + (k + 1) * P], idf[:, :])
                last.then_inc(S["aggt_back"], 1)

            def h3_product(g):
                for k in range(TC):
                    t = TC * g + k
                    last = nc.tensor.matmul(ps[:, 4 + g, k * P:(k + 1) * P], ht[:, t * P:(t + 1) * P],
                                            w3_sb[:, :, :], start=True, stop=True)
                if g % 2:
                    last.then_inc(S["h3_ready"], 1)

            through(8, 2 * NC, h3_product)

            def sums_3(g, j0):
                for h in range(2):
                    t = 2 * g + h
                    for j in range(j0, j0 + 8):
                        last = nc.tensor.matmul(ps[:, g % 4, h * PW:(h + 1) * PW], mask8[:, j, t * P:(t + 1) * P],
                                                parts3[:, j, :], start=(j == 0 and h == 0), stop=(j == T - 1),
                                                skip_group_check=True)
                if j0:
                    last.then_inc(S["sum3_ready"], 1)

            pe.wait_ge(S["parts_ready"], 1)
            for g in range(4):
                sums_3(g, 0)
            pe.wait_ge(S["parts_ready"], 2)
            for g in range(4):
                sums_3(g, 8)
            for g in range(4, 8):
                pe.wait_ge(S["sum3_read"], g - 3)
                sums_3(g, 0)
                sums_3(g, 8)

        @block.vector
        def _(v):
            dve = nc.vector
            done = [0]

            def step(ins):
                done[0] += 1
                ins.then_inc(S["step"], 1)
                v.wait_ge(S["step"], done[0])

            def centre(src, a=slice(0, T)):
                n = a.stop - a.start
                step(dve.tensor_reduce(st[:, 0, a], src, X, ALU.add))
                step(dve.tensor_scalar(st[:, 1, a], st[:, 0, a], -1.0 / D, None, ALU.mult))
                step(dve.tensor_tensor(xc[:, a, :], src, over_features(st[:, 1, a], n), ALU.add))
                step(dve.tensor_tensor(sq[:, a, :], xc[:, a, :], xc[:, a, :], ALU.mult))
                step(dve.tensor_reduce(st[:, 0, a], sq[:, a, :], X, ALU.add))

            def layer_norm(n, signal=None, a=slice(0, T)):
                centre(xs[:, a, :], a)
                dve.tensor_scalar(st[:, 2, a], st[:, 0, a], 1.0 / D, LN_EPS, ALU.mult, ALU.add)\
                    .then_inc(S["var_ready"], 1)
                v.wait_ge(S["std_ready"], n)
                step(dve.reciprocal(st[:, 4, a], st[:, 3, a]))
                if not signal:
                    step(dve.scalar_tensor_tensor(h_feat[:, a, :], xc[:, a, :], 0.0,
                                                  over_features(st[:, 4, a], a.stop - a.start), ALU.max, ALU.mult))
                    return
                for g in range(NC):
                    q = slice(TC * g, TC * g + TC)
                    dve.scalar_tensor_tensor(h_feat[:, q, :], xc[:, q, :], 0.0, over_features(st[:, 4, q], TC),
                                             ALU.max, ALU.mult).then_inc(S[signal], 1)

            v.wait_ge(S["x_in"], 16)
            centre(xs[:, :, :])
            step(dve.tensor_scalar(stat(2), stat(0), 1.0 / D, LN_EPS, ALU.mult, ALU.add))
            dve.tensor_scalar(xc, xc, 0.0, None, ALU.max)
            step(dve.reciprocal(stat(4), stat(2)))
            centre(xc)
            step(dve.tensor_tensor(stat(0), stat(0), stat(4), ALU.mult))
            step(dve.tensor_scalar(stat(0), stat(0), EPS0 * EPS0, None, ALU.max))
            step(dve.reciprocal(stat(1), stat(0)))
            dve.tensor_tensor(stat(2), stat(1), stat(4), ALU.mult).then_inc(S["var_ready"], 1)
            v.wait_ge(S["std_ready"], 1)
            dve.tensor_tensor(h_feat, xc, over_features(stat(3)), ALU.mult).then_inc(S["feat_ready"], 1)
            v.wait_ge(S["w_in"], W_IN)
            v.wait_ge(S["const_set"], 11)
            step(dve.tensor_copy(wk_rep[0:D, :, :], wkq[:, 0:1, :].to_broadcast([D, 9, EMB])))
            step(dve.tensor_copy(idb[:, :], idf[:, :]))
            dve.tensor_copy(wq_rep[0:D, :, :], wkq[:, 1:2, :].to_broadcast([D, 9, EMB])).then_inc(S["wa_set"], 1)
            for j in CAST["v"]:
                v.wait_ge(adj_in[j], 16)
                dve.tensor_copy(mask8[:, j, :], adj_stage[:, j, :], saturate=False).then_inc(S["cast_v"], 1)
            v.wait_ge(S["feat_ready"], 1)
            for m in range(2):
                for n, part in enumerate((k_part, q_part)):
                    v.wait_ge(S["rnd_ready"], 2 * m + n + 1)
                    src = ps[0:KP, 4 * n:4 * n + 4, :]
                    dst = part[0:KP, :].rearrange("p (b c) -> p b c", b=NC) if m else src
                    dve.scalar_tensor_tensor(dst, rounded[n][0:KP, :].rearrange("p (b c) -> p b c", b=NC),
                                             sel_sb[0:KP, 2 * n + m:2 * n + m + 1], src,
                                             ALU.mult, ALU.add).then_inc(S["part_ready"], 1)

            def row_max(c):
                for g in range(8 * c, 8 * c + 8):
                    if c >= 2 and g % 8 in MASK_V[c - 2]:
                        mask_weights(c - 2, g % 8)
                    v.wait_ge(S["gmax_ready"], g + 1)
                    b = 2 * (g % 2)
                    dve.tensor_reduce(rowmax[:, g // 2, g % 2:g % 2 + 1], ps[:, b:b + 2, :],
                                      mybir.AxisListType.XY, ALU.max).then_inc(S["gmax_read"], 1)
                v.wait_ge(S["gmax_read"], 8 * c + 8)
                a = slice(TC * c, TC * c + TC)
                step(dve.tensor_reduce(st[:, 5, a], rowmax[:, a, :], X, ALU.max))
                step(dve.tensor_copy(m_parts[:, a, 0], st[:, 5, a]))
                step(dve.tensor_tensor(st[:, 5, a], st[:, 5, a], m_parts[:, a, 0], ALU.subtract))
                step(dve.tensor_copy(m_parts[:, a, 1], st[:, 5, a]))
                dve.tensor_tensor(m_parts[:, a, 2], st[:, 5, a], m_parts[:, a, 1], ALU.subtract)\
                    .then_inc(S["mcol_ready"], 1)

            def mask_weights(c, g):
                v.wait_ge(S["exp_ready"], T * c + 2 * g + 2)
                e = attn[:, 2 * g:2 * g + 2, c * CH:(c + 1) * CH]
                dve.tensor_tensor(e, e, mask8[:, 2 * g:2 * g + 2, c * CH:(c + 1) * CH], ALU.mult)\
                    .then_inc(S["masked_v"], 1)

            def pair_turned(n):
                v.wait_ge(S["u_turned"], n + 1)
                a = slice(8 * (n % 2), 8 * (n % 2) + 8)
                u = u_buf[(n // 2) % 2][:, a, :].rearrange("p (h k) f -> p k h f", h=2)
                acc = ps[:, 2 + n % 2, :].rearrange("p (k h f) -> p k h f", k=TC, h=2)
                weight = st[:, 6, a].rearrange("p (h k) -> p k h", h=2)
                if n >= 2:
                    dve.tensor_tensor(u, acc, weight.unsqueeze(3).to_broadcast([P, TC, 2, D]), ALU.mult)\
                        .then_inc(S["u_ready"], 1)
                    return
                step(dve.reciprocal(weight, acc[:, :, :, D - 1]))
                step(dve.tensor_tensor(u[:, :, :, 1:D], acc[:, :, :, 0:D - 1],
                                       weight.unsqueeze(3).to_broadcast([P, TC, 2, D - 1]), ALU.mult))
                step(dve.tensor_reduce(st[:, 7, a], u_buf[0][:, a, 1:D], X, ALU.add))
                dve.tensor_scalar(u_buf[0][:, a, 0], st[:, 7, a], -1.0, None, ALU.mult).then_inc(S["u_ready"], 1)

            def add_u(k, factor, a=slice(0, T)):
                step(dve.scalar_tensor_tensor(xs[:, a, :], u_buf[(k + 1) % 2][:, a, :], factor, xs[:, a, :],
                                              ALU.mult, ALU.add))

            def features_1(half):
                a = slice(half * T // 2, (half + 1) * T // 2)
                v.wait_ge(S["u_ready"], 7 + half)
                add_u(4, 1.0 / 6.0, a)
                layer_norm(2 + half, a=a)
                dve.tensor_scalar(feat_a[half][:, :, 0:D], h_feat[:, a, :], -2.0, None, ALU.mult)
                step(dve.tensor_tensor(sq[:, a, :], h_feat[:, a, :], h_feat[:, a, :], ALU.mult))
                step(dve.tensor_reduce(st[:, 5, a], sq[:, a, :], X, ALU.add))
                dve.tensor_copy(feat[:, a, D + 1], st[:, 5, a])
                dve.tensor_copy(feat_a[half][:, :, D], st[:, 5, a])
                dve.memset(feat_a[half][:, :, D + 1:D + 2], 1.0)
                dve.tensor_scalar(st[:, 6, a], st[:, 5, a], -1.0, 1.0, ALU.mult, ALU.add)\
                    .then_inc(S["feat_ready"], 1)

            for c in range(NC):
                row_max(c)
            for c in (2, 3):
                for g in MASK_V[c]:
                    mask_weights(c, g)
            for n in range(8):
                pair_turned(n)
                if n == 2:
                    add_u(1, 1.0)
                if n == 4:
                    add_u(2, 0.5)
                if n >= 6:
                    features_1(n - 6)

            for g in (2, 3):
                v.wait_ge(S["pad_set"], 4)
                v.wait_ge(S["operand_turned"], 2 * g + 2)
                dve.tensor_copy(xa[0:AUG, g * CH:(g + 1) * CH], ps[0:AUG, 2 * (g % 2) + 1, :])\
                    .then_inc(S["xa_late"], 1)
            v.wait_ge(S["brow_set"], 2)

            for c in range(NCH + LO_LAG):
                if c < NCH:
                    r = c % R
                    v.wait_ge(S["gram_ready"], c + 1)
                    for s, n, j, i in runs(CHUNKS[c], True):
                        last = dve.scalar_tensor_tensor(ring["den"][r][:, s * P:(s + n) * P], b_row[:, i * P:(i + n) * P],
                                                        st[:, 6, j:j + 1], ps[:, c % 2, s * P:(s + n) * P],
                                                        ALU.mult, ALU.add)
                    last.then_inc(S["den_ready"], 1)
                if 1 <= c <= NCH:
                    b = c - 1
                    v.wait_ge(S["gram_read"], b + 1)
                    dve.tensor_tensor(ring["prod"][b % R], ring["dist"][b % R], ring["den"][b % R], ALU.mult)\
                        .then_inc(S["product_ready"], 1)
                if c < NCH:
                    v.wait_ge(S["den_ready"], c + 1)
                    dve.tensor_scalar(ring["den"][r], ring["den"][r], EPS1, UMAX * UMAX, ALU.max, ALU.mult)\
                        .then_inc(S["den_held"], 1)
                if W_LAG <= c < NCH + W_LAG:
                    b = c - W_LAG
                    if on_vector(b):
                        v.wait_ge(S["ln_ready"], b + 1)
                        step(dve.tensor_tensor(ring["atn"][b % R], ring["atn"][b % R], ring["dist"][b % R],
                                               ALU.subtract))
                    else:
                        v.wait_ge(S["atn_ready"], sum(not on_vector(k) for k in range(b + 1)))
                    if b >= R:
                        v.wait_ge(S["wup_ready"], wup_count[b - R + 1])
                        v.wait_ge(S["wt_ready"], b - R + 1)
                    dve.tensor_tensor(ring["w"][b % R], ring["atn"][b % R], ring["inv_s"][b % R], ALU.mult)\
                        .then_inc(S["w_ready"], 1)
                if c < NCH:
                    v.wait_ge(S["den_held"], c + 1)
                    dve.scalar_tensor_tensor(ring["dist"][r], ps[:, c % 2, :], DMIN, ring["den"][r],
                                             ALU.max, ALU.min).then_inc(S["gram_read"], 1)
                if c >= LO_LAG:
                    b = c - LO_LAG
                    v.wait_ge(S["wt_ready"], b + 1)
                    if b >= R:
                        v.wait_ge(S["sum1_done"], b - R + 1)
                    rr = runs(CHUNKS[b], False)
                    for k, (s, n, j, i) in enumerate(rr):
                        last = dve.tensor_tensor(
                            ring["w_lo"][b % R][:, s * P:(s + n) * P].rearrange("p (t i) -> p t i", t=n),
                            ps[:, 2 + b % 2, s * P:(s + n) * P].rearrange("p (t i) -> p t i", t=n),
                            mask8[:, i:i + n, j * P:(j + 1) * P], ALU.mult)
                    if rr:
                        last.then_inc(S["wlo_ready"], 1)
                    else:
                        v.sem_inc(S["wlo_ready"], 1)
                if W_LAG <= c < NCH + W_LAG and c - W_LAG >= NCH - LATE:
                    b = c - W_LAG
                    v.wait_ge(S["w_ready"], b + 1)
                    v.wait_ge(S["sum1_done"], b - R + 1)
                    for s, n, j, i in runs(CHUNKS[b], True):
                        last = dve.tensor_tensor(ring["w_up"][b % R][:, s * P:(s + n) * P],
                                                 ring["w"][b % R][:, s * P:(s + n) * P],
                                                 mask8[:, j, i * P:(i + n) * P], ALU.mult)
                    last.then_inc(S["wup_late"], 1)

            agg = by_tile(0, AUG)
            v.wait_ge(S["aggt_back"], 1)
            dve.tensor_reduce(stat(1), agg[:, :, D:AUG], X, ALU.add)
            dve.tensor_scalar(stat(14), stat(6), 0.5, None, ALU.mult)
            dve.tensor_scalar(stat(9), stat(6), EPS1, None, ALU.max)
            step(dve.tensor_tensor(sq, h_feat, agg[:, :, 0:D], ALU.mult))
            step(dve.tensor_reduce(stat(0), sq, X, ALU.add))
            dve.scalar_tensor_tensor(stat(2), stat(1), 0.5, stat(0), ALU.mult, ALU.subtract)
            dve.tensor_tensor(stat(13), stat(14), stat(0), ALU.mult)
            step(dve.tensor_tensor(xc, agg[:, :, 0:D], over_features(stat(14)), ALU.mult))
            step(dve.tensor_tensor(sq, h_feat, over_features(stat(2)), ALU.mult))
            step(dve.tensor_tensor(xc, xc, sq, ALU.subtract))
            step(dve.tensor_tensor(sq, xc, xc, ALU.mult))
            dve.tensor_tensor(stat(17), stat(2), stat(5), ALU.mult)
            dve.reciprocal(stat(14), stat(9))
            step(dve.tensor_reduce(stat(12), sq, X, ALU.add))
            dve.tensor_scalar(stat(7), stat(12), 1e-30, None, ALU.max).then_inc(S["square_ready"], 1)
            dve.tensor_tensor(stat(13), stat(13), stat(17), ALU.subtract)
            v.wait_ge(S["norm_ready"], 1)
            step(dve.tensor_tensor(stat(8), stat(8), stat(9), ALU.mult))
            step(dve.tensor_scalar(stat(8), stat(8), EPS1, None, ALU.max))
            dve.tensor_tensor(stat(10), stat(8), stat(14), ALU.mult).then_inc(S["angle_ready"], 1)
            step(dve.reciprocal(stat(15), stat(8)))
            step(dve.tensor_tensor(stat(15), stat(15), stat(9), ALU.mult))
            v.wait_ge(S["tanh_ready"], 1)
            step(dve.tensor_tensor(stat(15), stat(15), stat(11), ALU.mult))
            dve.tensor_tensor(stat(13), stat(13), stat(15), ALU.mult)
            dve.tensor_tensor(stat(6), stat(6), stat(15), ALU.mult)
            step(dve.tensor_tensor(stat(16), stat(15), stat(15), ALU.mult))
            dve.tensor_scalar(stat(13), stat(13), 2.0, 1.0, ALU.mult, ALU.add)
            step(dve.tensor_tensor(stat(16), stat(16), stat(12), ALU.mult))
            step(dve.tensor_tensor(stat(0), stat(5), stat(16), ALU.mult))
            step(dve.tensor_tensor(stat(0), stat(0), stat(13), ALU.add))
            dve.tensor_tensor(stat(13), stat(13), stat(16), ALU.add)
            step(dve.tensor_scalar(stat(0), stat(0), EPS1, None, ALU.max))
            step(dve.reciprocal(stat(1), stat(0)))
            dve.tensor_tensor(stat(13), stat(13), stat(1), ALU.mult).then_inc(S["coef_x"], 1)
            step(dve.tensor_tensor(stat(6), stat(6), stat(1), ALU.mult))
            step(dve.tensor_tensor(xc, xc, over_features(stat(6)), ALU.mult))
            step(dve.tensor_tensor(xs[:, :, :], xs[:, :, :], xc, ALU.add))
            v.wait_ge(S["along_x"], 1)
            step(dve.tensor_tensor(xs[:, :, :], xs[:, :, :], sq, ALU.add))

            layer_norm(4, "feat_ready")
            v.wait_ge(S["wa_ready"], 1)
            dve.tensor_copy(w2_sb[0:D, D:D + 2], ps[0:D, 4, 0:2]).then_inc(S["wa_set"], 1)
            v.wait_ge(S["wh_ready"], 1)
            wh_ps = by_tile(4, AUG)
            dve.tensor_copy(stat(16), wh_ps[:, :, D + 1])
            dve.tensor_reduce(st[:, 18, 0:1], wh_ps[:, :, D + 1:AUG], mybir.AxisListType.XY, ALU.min)\
                .then_inc(S["min_ready"], 1)
            dve.tensor_copy(stat(15), wh_ps[:, :, D])
            v.wait_ge(S["min_t"], 1)
            dve.tensor_reduce(st[0:1, 18, 1:2], ps[0:1, 0, 0:P], X, ALU.min).then_inc(S["min_r"], 1)
            dve.tensor_copy(wh, wh_ps[:, :, 0:D])
            v.wait_ge(S["min_b"], 1)
            step(dve.tensor_copy(st[:, 18, 2:3], ps[:, 0, P:P + 1]))
            dve.tensor_scalar(stat(17), stat(16), ALPHA, None, ALU.mult)
            dve.tensor_scalar(stat(19), stat(16), 1.0 - ALPHA, None, ALU.mult)
            dve.tensor_scalar(stat(20), stat(15), 1.0 - ALPHA, None, ALU.mult).then_inc(S["spread_ready"], 1)
            dve.tensor_scalar(stat(22), stat(16), st[:, 18, 2:3], None, ALU.subtract).then_inc(S["above_ready"], 1)
            v.wait_ge(S["above_ready"], 1)
            step(dve.tensor_scalar(best, mask8[:, 0, :], st[:, 22, 0:1], None, ALU.mult))
            for j in range(1, T - BEST_G):
                step(dve.scalar_tensor_tensor(best, mask8[:, j, :], st[:, 22, j:j + 1], best, ALU.mult, ALU.max))
            v.wait_ge(S["best_g"], 3)
            step(dve.tensor_tensor(best, best, p_ring[0], ALU.max))
            v.wait_ge(S["best_g"], 4)
            for c in range(NC):
                a = slice(c * CH, (c + 1) * CH)
                dve.tensor_tensor(best[:, a], best[:, a], p_ring[2][:, a], ALU.max).then_inc(S["best_ready"], 1)
            for c in range(NC):
                v.wait_ge(S["best_turned"], c + 1)
                ins = dve.tensor_reduce(st[:, 0, TC * c:TC * c + TC],
                                        ps[:, c, :].rearrange("p (k i) -> p k i", k=TC), X, ALU.max)
            step(ins)
            step(dve.tensor_scalar(stat(0), stat(0), st[:, 18, 2:3], None, ALU.add))
            step(dve.tensor_tensor(stat(0), stat(0), stat(15), ALU.add))
            step(dve.scalar_tensor_tensor(stat(0), stat(0), ALPHA, stat(0), ALU.mult, ALU.max))
            dve.scalar_tensor_tensor(stat(21), stat(15), ALPHA, stat(0), ALU.mult, ALU.subtract)\
                .then_inc(S["m_ready"], 1)
            v.wait_ge(S["row1_set"], 1)
            for c in range(NC):
                v.wait_ge(S["row2_set"], c + 1)
                a = slice(c * CH, (c + 1) * CH)
                ins = dve.tensor_tensor(row_1[:, a], row_1[:, a], row_2[:, a], ALU.add)
            step(ins)
            for j in range(T + PM_LAG):
                if j < T:
                    if j >= R2:
                        v.wait_ge(S["sum2_done"], j - R2 + 1)
                    dve.scalar_tensor_tensor(p_ring[j % R2], row_1, st[:, 19, j:j + 1], row_2, ALU.add, ALU.max)\
                        .then_inc(S["z_ready"], 1)
                b = 0 if j == 1 else j - PM_LAG
                if (b > 0 or j == 1) and b not in POOL_J:
                    v.wait_ge(S["exp2_ready"], b + 1)
                    dve.scalar_tensor_tensor(p_ring[b % R2], mask8[:, b, :], 2.0, p_ring[b % R2],
                                             ALU.mult, ALU.min).then_inc(S["masked2_ready"], 1)
            v.wait_ge(S["aggt_back"], 2)
            weights = ps[:, 2, :].rearrange("p (k c x) -> p c k x", k=TC, c=NC)[:, :, :, 0]
            step(dve.reciprocal(stat(0).rearrange("p (c k) -> p c k", c=NC), weights))
            for n in range(2):
                v.wait_ge(S["aggt_back"], 3 + n)
                a = slice(8 * n, 8 * n + 8)
                step(dve.tensor_tensor(xc[:, a, :].rearrange("p (h k) f -> p k h f", h=2),
                                       ps[:, n, :].rearrange("p (k h f) -> p k h f", k=TC, h=2),
                                       st[:, 0, a].rearrange("p (h k) -> p k h", h=2).unsqueeze(3)
                                       .to_broadcast([P, TC, 2, D]), ALU.mult))
            dve.tensor_scalar(sq, xc, 0.0, None, ALU.min).then_inc(S["elu_ready"], 1)
            step(dve.scalar_tensor_tensor(xs[:, :, :], xc, 0.0, xs[:, :, :], ALU.max, ALU.add))
            v.wait_ge(S["elu_exp"], 1)
            step(dve.scalar_tensor_tensor(xs[:, :, :], sq, -1.0, xs[:, :, :], ALU.add, ALU.add))

            layer_norm(5, "feat_ready")
            src = by_tile(4)
            dve.memset(parts3[:, :, 3 * D:PW], 1.0)
            for n in range(2):
                a = slice(8 * n, 8 * n + 8)
                v.wait_ge(S["h3_ready"], n + 1)
                step(dve.tensor_copy(parts3[:, a, 0:D], src[:, a, 0:D]))
                step(dve.tensor_tensor(r3[:, a, :], src[:, a, 0:D], parts3[:, a, 0:D], ALU.subtract))
                step(dve.tensor_copy(parts3[:, a, D:2 * D], r3[:, a, :]))
                dve.tensor_tensor(parts3[:, a, 2 * D:3 * D], r3[:, a, :], parts3[:, a, D:2 * D], ALU.subtract)\
                    .then_inc(S["parts_ready"], 1)
            step(dve.tensor_tensor(self3, src[:, :, D:2 * D], xs[:, :, :], ALU.add))
            step(dve.tensor_tensor(self3, self3, bias_sb[:, :].unsqueeze(1).to_broadcast([P, T, D]), ALU.add))
            for g in range(T // 2):
                a = slice(2 * g, 2 * g + 2)
                v.wait_ge(S["sum3_ready"], g + 1)
                acc = ps[:, g % 4, 0:2 * PW].rearrange("p (t f) -> p t f", t=2)
                step(dve.reciprocal(st[:, 23, a], acc[:, :, 3 * D]))
                dve.tensor_reduce(r3[:, a, :], acc[:, :, 0:3 * D].rearrange("p t (s f) -> p t f s", s=3), X, ALU.add)\
                    .then_inc(S["sum3_read"], 1)
                v.wait_ge(S["sum3_read"], g + 1)
                step(dve.tensor_tensor(r3[:, a, :], r3[:, a, :], st[:, 23, a].unsqueeze(2).to_broadcast([P, 2, D]),
                                       ALU.mult))
                ins = dve.tensor_tensor(xs[:, a, :], r3[:, a, :], self3[:, a, :], ALU.add)
                if g % 4 == 3:
                    ins.then_inc(S["y_ready"], 1)


def kernel(x, adj, L0_gnn_w_k, L0_gnn_w_q, L2_gnn_W, L2_gnn_a, L3_gnn_weight, L3_gnn_bias):
    import numpy as np
    import concourse.bacc as bacc
    from concourse.bass_utils import run_bass_kernel_spmd as run

    sel = np.zeros((P, 4), np.float32)
    for r in range(KP):
        a, b = r // EMB // 3, r // EMB % 3
        sel[r] = (-(a > 0), -(a > 1), -(b > 0), -(b > 1))
    f = np.asarray
    arrays = {
        "x": np.ascontiguousarray(f(x)),
        "adj_t": np.ascontiguousarray(f(adj).T),
        "w_k": np.ascontiguousarray(f(L0_gnn_w_k)),
        "w_q": np.ascontiguousarray(f(L0_gnn_w_q)),
        "w2": np.ascontiguousarray(f(L2_gnn_W)),
        "w2_t": np.ascontiguousarray(f(L2_gnn_W).T),
        "a2": np.ascontiguousarray(f(L2_gnn_a).reshape(2, D).T),
        "w3": np.ascontiguousarray(f(L3_gnn_weight)),
        "bias3": np.ascontiguousarray(f(L3_gnn_bias)),
        "sel": sel,
        "ident": np.eye(P, dtype=np.float32),
    }
    nc = bacc.Bacc("TRN2", target_bir_lowering=False, num_devices=1)
    args = [nc.dram_tensor("in_" + n, a.shape, mybir.dt.from_np(a.dtype), kind="ExternalInput").ap()
            for n, a in arrays.items()]
    out = nc.dram_tensor("out", (N, D), F32, kind="ExternalOutput").ap()
    build(nc, *args, out)
    r = run(nc, [{"in_" + n: a for n, a in arrays.items()}], core_ids=[0])
    return r.results[0]["out"]
```
